# Optimizing a Trainium2 kernel written in Bass

```python
import numpy as np
import jax
import jax.numpy as jnp

def _softmax(x, axis=-1):
    return jax.nn.softmax(x, axis=axis)

def _gelu(x):
    return jax.nn.gelu(x, approximate=True)

def _silu(x):
    return jax.nn.silu(x)

def _sigmoid(x):
    return jax.nn.sigmoid(x)

def _layernorm(x, axis=-1, eps=1e-05):
    m = jnp.mean(x, axis=axis, keepdims=True)
    v = jnp.var(x, axis=axis, keepdims=True)
    return (x - m) / jnp.sqrt(v + eps)

def _scatter_add(tgt, idx, src, axis=0):
    return tgt.at[idx].add(src)

def _segment_sum(src, seg, n):
    return jax.ops.segment_sum(src, seg, n)
kernel_name = 'mk_vit_tower_d1_tok_img768_r4_7be031'

def setup_inputs(seed: int=0):
    np.random.seed(seed)
    _w = jnp.asarray

    def _rec_inputs():
        import jax
        import jax.numpy as jnp
        _rk = jax.random.key(seed)
        x = -0.000356955 + 1 * jax.random.normal(jax.random.fold_in(_rk, 1), (8, 3, 128, 128), jnp.float32)
        return x
    x = _rec_inputs()

    def _L0_tok_setup():
        import jax, jax.numpy as jnp
        import numpy as np
        PATCH = 16
        P2 = PATCH * PATCH
        C_OUT = 192
        key = jax.random.key(seed)
        k1, k2, k3 = jax.random.split(key, 3)
        img = jax.random.normal(k1, (128, 3, 224, 224), dtype=jnp.float32)
        in_dim = P2 * 3
        bound = 1.0 / np.sqrt(in_dim)
        W = jax.random.uniform(k2, (C_OUT, in_dim), minval=-bound, maxval=bound, dtype=jnp.float32)
        b = jax.random.uniform(k3, (C_OUT,), minval=-bound, maxval=bound, dtype=jnp.float32)
        return {'img': img, 'W': W, 'b': b}
    _L0_tok_all = _L0_tok_setup()
    _L0_tok_in = {k: v for k, v in _L0_tok_all.items() if k in ('W', 'b')}
    del _L0_tok_all

    def _L0_attn_setup():
        import jax, jax.numpy as jnp
        import numpy as np
        N_DIM = 192
        HIDDEN_DIM = 192
        BATCH = 4
        SEQ = 512
        key = jax.random.key(seed)
        ks = jax.random.split(key, 9)
        s_in = 1.0 / np.sqrt(N_DIM)
        s_h = 1.0 / np.sqrt(HIDDEN_DIM)
        return {'x': jax.random.normal(ks[0], (BATCH, SEQ, N_DIM), dtype=jnp.float32), 'wq': jax.random.uniform(ks[1], (HIDDEN_DIM, N_DIM), jnp.float32, -s_in, s_in), 'bq': jax.random.uniform(ks[2], (HIDDEN_DIM,), jnp.float32, -s_in, s_in), 'wk': jax.random.uniform(ks[3], (HIDDEN_DIM, N_DIM), jnp.float32, -s_in, s_in), 'bk': jax.random.uniform(ks[4], (HIDDEN_DIM,), jnp.float32, -s_in, s_in), 'wv': jax.random.uniform(ks[5], (HIDDEN_DIM, N_DIM), jnp.float32, -s_in, s_in), 'bv': jax.random.uniform(ks[6], (HIDDEN_DIM,), jnp.float32, -s_in, s_in), 'wo': jax.random.uniform(ks[7], (N_DIM, HIDDEN_DIM), jnp.float32, -s_h, s_h), 'bo': jax.random.uniform(ks[8], (N_DIM,), jnp.float32, -s_h, s_h)}
    _L0_attn_all = _L0_attn_setup()
    _L0_attn_in = {k: v for k, v in _L0_attn_all.items() if k in ('wq', 'bq', 'wk', 'bk', 'wv', 'bv', 'wo', 'bo')}
    del _L0_attn_all

    def _L0_ffn_setup():
        import jax, jax.numpy as jnp
        import numpy as np
        B, L, D = (4, 256, 192)
        E, S, H = (32, 32, 768)
        EPS = 1e-12

        def _l2norm(v, axis):
            n = jnp.sqrt(jnp.sum(v * v, axis=axis, keepdims=True))
            return v / jnp.maximum(n, EPS)
        key = jax.random.key(seed)
        ks = jax.random.split(key, 6)
        x = jax.random.normal(ks[0], (B, L, D), dtype=jnp.float32)
        phi = jax.random.normal(ks[1], (D, E, S), dtype=jnp.float32) / np.sqrt(D)
        scale = jnp.ones((1,), dtype=jnp.float32)
        w1 = jax.random.normal(ks[2], (E, D, H), dtype=jnp.float32) / np.sqrt(D)
        b1 = jax.random.normal(ks[3], (E, H), dtype=jnp.float32) * 0.01
        w2 = jax.random.normal(ks[4], (E, H, D), dtype=jnp.float32) / np.sqrt(H)
        b2 = jax.random.normal(ks[5], (E, D), dtype=jnp.float32) * 0.01
        return {'x': x, 'phi': phi, 'scale': scale, 'w1': w1, 'b1': b1, 'w2': w2, 'b2': b2}
    _L0_ffn_all = _L0_ffn_setup()
    _L0_ffn_in = {k: v for k, v in _L0_ffn_all.items() if k in ('phi', 'scale', 'w1', 'b1', 'w2', 'b2')}
    del _L0_ffn_all
    return {'x': x, 'L0_tok_W': _L0_tok_in['W'], 'L0_tok_b': _L0_tok_in['b'], 'L0_attn_wq': _L0_attn_in['wq'], 'L0_attn_bq': _L0_attn_in['bq'], 'L0_attn_wk': _L0_attn_in['wk'], 'L0_attn_bk': _L0_attn_in['bk'], 'L0_attn_wv': _L0_attn_in['wv'], 'L0_attn_bv': _L0_attn_in['bv'], 'L0_attn_wo': _L0_attn_in['wo'], 'L0_attn_bo': _L0_attn_in['bo'], 'L0_ffn_phi': _L0_ffn_in['phi'], 'L0_ffn_scale': _L0_ffn_in['scale'], 'L0_ffn_w1': _L0_ffn_in['w1'], 'L0_ffn_b1': _L0_ffn_in['b1'], 'L0_ffn_w2': _L0_ffn_in['w2'], 'L0_ffn_b2': _L0_ffn_in['b2']}

def reference(x, L0_tok_W, L0_tok_b, L0_attn_wq, L0_attn_bq, L0_attn_wk, L0_attn_bk, L0_attn_wv, L0_attn_bv, L0_attn_wo, L0_attn_bo, L0_ffn_phi, L0_ffn_scale, L0_ffn_w1, L0_ffn_b1, L0_ffn_w2, L0_ffn_b2):
    import jax
    import jax.numpy as jnp

    def _L0_tok_ref(img, W, b):
        import jax, jax.numpy as jnp
        import numpy as np
        PATCH = 16
        P2 = PATCH * PATCH
        C_OUT = 192
        N, C, H, Wd = img.shape
        S = H * Wd // P2
        x = img.reshape(N, C, S, P2)
        x = jnp.transpose(x, (0, 2, 1, 3)).reshape(N, S, C * P2)
        return jnp.einsum('nsd,cd->nsc', x, W) + b

    def _L0_attn_ref(x, wq, bq, wk, bk, wv, bv, wo, bo):
        import jax, jax.numpy as jnp
        import numpy as np
        N_DIM = 192
        HIDDEN_DIM = 192
        BATCH = 4
        SEQ = 512
        q = jnp.einsum('bsd,hd->bsh', x, wq) + bq
        k = jnp.einsum('bsd,hd->bsh', x, wk) + bk
        v = jnp.einsum('bsd,hd->bsh', x, wv) + bv
        scores = jnp.einsum('bqh,bkh->bqk', q, k)
        attn = jax.nn.softmax(scores, axis=-1)
        y = jnp.einsum('bqk,bkh->bqh', attn, v)
        out = jnp.einsum('bsh,dh->bsd', y, wo) + bo
        return out

    def _L0_ffn_ref(x, phi, scale, w1, b1, w2, b2):
        import jax, jax.numpy as jnp
        import numpy as np
        B, L, D = (4, 256, 192)
        E, S, H = (32, 32, 768)
        EPS = 1e-12

        def _l2norm(v, axis):
            n = jnp.sqrt(jnp.sum(v * v, axis=axis, keepdims=True))
            return v / jnp.maximum(n, EPS)
        b, l, d = x.shape
        xn = _l2norm(x, axis=2)
        phin = scale * _l2norm(phi, axis=0)
        logits = jnp.einsum('bld,des->bles', xn, phin)
        d_w = jax.nn.softmax(logits, axis=-1)
        c_w = jax.nn.softmax(logits.reshape(b, l, E * S), axis=-1)
        slots = jnp.einsum('bld,bles->besd', xn, d_w)
        h = jax.nn.gelu(jnp.einsum('besd,edh->besh', slots, w1) + b1[:, None, :], approximate=False)
        eo = jnp.einsum('besh,ehd->besd', h, w2) + b2[:, None, :]
        eo = eo.reshape(b, E * S, d)
        return jnp.einsum('bkd,blk->bld', eo, c_w)
    h = _L0_tok_ref(x, L0_tok_W, L0_tok_b)
    h = h + _L0_attn_ref(_layernorm(h, axis=-1), L0_attn_wq, L0_attn_bq, L0_attn_wk, L0_attn_bk, L0_attn_wv, L0_attn_bv, L0_attn_wo, L0_attn_bo)
    h = h + _L0_ffn_ref(_layernorm(h, axis=-1), L0_ffn_phi, L0_ffn_scale, L0_ffn_w1, L0_ffn_b1, L0_ffn_w2, L0_ffn_b2)
    return h

_drawn_inputs = setup_inputs


def setup_inputs(seed=0):
    import zlib

    import numpy as np

    out = dict(_drawn_inputs(seed))
    spreads = {}
    factors = {'L0_attn_bk': 64.0,
     'L0_ffn_phi': 64.0,
     'L0_ffn_w1': 8.0,
     'L0_ffn_b1': 8.0,
     'L0_ffn_w2': 8.0,
     'L0_ffn_b2': 22.076}
    for name, (base, spread) in spreads.items():
        noise = np.random.default_rng([zlib.crc32(name.encode()), seed]).standard_normal(out[name].shape)
        drawn = base * np.exp(spread * noise) if base else spread * noise
        out[name] = jnp.asarray(drawn.astype(out[name].dtype))
    for name, factor in factors.items():
        out[name] = (out[name] * factor).astype(out[name].dtype)
    return out
```

```python
import concourse.bass as bass
from concourse import mybir
from contextlib import ExitStack

F32 = mybir.dt.float32
F32R = mybir.dt.float32r
ALU = mybir.AluOpType
ACT = mybir.ActivationFunctionType
AX = mybir.AxisListType

P = 128
B, L, D = 8, 64, 192
DC = D - P
NT = B * L // P
PK = 6
E, S, H = 32, 32, 768
HT = H // P
ROWS = B * S
EG = 4
NG = E // EG
GC = EG * S
EO_IN = 16 * B
LN_EPS = 1e-5
L2_EPS2 = 1e-24


def vit_block(nc, xT, wtokT, rowbias, wattnAB, wattnC, bqkAB, bqkC, phi, scale, b2, wA, wC, out):
    out_v = out.rearrange("b l d -> (b l) d").rearrange("(t p) d -> p t d", p=P)

    ctx = ExitStack()
    with ctx:
        def sb(name, shape, dt=F32):
            return ctx.enter_context(nc.sbuf_tensor(name, shape, dt))

        def sem(name):
            return ctx.enter_context(nc.semaphore(name))

        rawA = sb("rawA", [P, EG, H + HT * D + HT])
        rawC = sb("rawC", [DC, EG, H])
        w1h = sb("w1h", [P, 2, H], F32R)
        w1l = sb("w1l", [P, 2, H], F32R)
        w1c = sb("w1c", [P, 2, H], F32R)
        w2s = sb("w2s", [P, 2, HT, 2 * D], F32R)
        xABh = sb("xABh", [P, EG, ROWS], F32R)
        xABl = sb("xABl", [P, EG, ROWS], F32R)
        xCh = sb("xCh", [P, EG, ROWS], F32R)
        xCl = sb("xCl", [P, EG, ROWS], F32R)
        hf = sb("hf", [P, 2 * HT * ROWS])
        hh = sb("hh", [P, 2, HT, ROWS], F32R)
        hl = sb("hl", [P, 2, HT, ROWS], F32R)
        eol = sb("eol", [P, 2, D])
        eot = sb("eot", [P, 2, D])
        eog = sb("eog", [P, B, D])
        cws = sb("cws", [P, NT, GC])
        cwT = sb("cwT", [P, NT * P])
        dw = sb("dw", [P, NT, E * S])
        gate = sb("gate", [P, NT, E])
        gateT = sb("gateT", [E, NT * P])
        xnp = sb("xnp", [P, B, D + DC])
        ident = sb("ident", [P, P])
        ones = sb("ones", [P, P])
        mhalf = sb("mhalf", [P, E * S // P])
        h = sb("h", [P, NT, D])
        xn = sb("xn", [P, NT, D])
        xT2 = sb("xT2", [P, 2, NT * P])
        v = sb("v", [P, NT, D])
        rb = sb("rb", [P, 3, D])
        wat = sb("wat", [P, 4, D])
        watC = sb("watC", [DC, 4, D])
        bqk = sb("bqk", [P, 2])
        bqk_c = sb("bqk_c", [DC, 2])
        phA = sb("phA", [P, E * S])
        phC = sb("phC", [DC, E * S])
        scl = sb("scl", [P, 1])
        b2s = sb("b2s", [E, D])
        dsc = sb("dsc", [P, 2, P])
        st = sb("st", [P, NT, 6])
        mv = sb("mv", [P, NT, 2])
        ve = sb("ve", [P, NT])
        rstd = sb("rstd", [P, NT])
        sq = sb("sq", [P, NT, D])
        ss = sb("ss", [P, NT])
        rn = sb("rn", [P, NT])
        pss = sb("pss", [P, E * S // P])
        pinv = sb("pinv", [P, E * S // P])
        nmx = sb("nmx", [P, NT])
        asum = sb("asum", [P, NT])
        arec = sb("arec", [P, NT])
        mE = sb("mE", [P, NT, E])
        nM = sb("nM", [P, NT])
        tE = sb("tE", [P, NT, E])
        sE = sb("sE", [P, NT, E])
        rE = sb("rE", [P, NT, E])
        uE = sb("uE", [P, NT, E])
        uS = sb("uS", [P, NT])
        ru = sb("ru", [P, NT])

        xTs = dw[:, 0:3, :].rearrange("p a n -> p (a n)").rearrange("p (k t) -> p k t", k=PK)
        phsq = dw[:, 3, :]
        wtk = eog[:, 0:PK, :]
        qA, kA = hf[:, 0:512], hf[:, 512:1024]
        qC, kC = hf[0:DC, 1024:1536], hf[0:DC, 1536:2048]
        yA, yC = hf[:, 2048:2560], hf[0:DC, 2560:3072]
        phsqC = hf[0:DC, 2048:3072]
        prob = cws
        probT = cwT

        R = ctx.enter_context(nc.psum_tensor("R", [P, 4, 512], F32))
        EO = ctx.enter_context(nc.psum_tensor("EO", [P, 2, 512], F32))
        Y = ctx.enter_context(nc.psum_tensor("Y", [P, 2, 512], F32))
        G = 3

        tok_in, bias_in, attn_in, phi_in = (sem(n) for n in ("tok_in", "bias_in", "attn_in", "phi_in"))
        w1_in = [sem(f"w1_in{s}") for s in range(EG)]
        w2_in = [sem(f"w2_in{s}") for s in range(EG)]
        eo_in = [sem(f"eo_in{s}") for s in range(EG)]
        out_done = sem("out_done")
        const_up, id_up = sem("const_up"), sem("id_up")
        tok_mm, h_up, ve_up, rstd_up, xn1_up = (sem(n) for n in ("tok_mm", "h_up", "ve_up", "rstd_up", "xn1_up"))
        t1_mm, x1T_up, qk_mm, v_mm, qk_up, v_up = (sem(n) for n in ("t1_mm", "x1T_up", "qk_mm", "v_mm", "qk_up", "v_up"))
        sc_mm, nmx_up, exp_up, prob_up, pT_mm, pT_up = (sem(n) for n in ("sc_mm", "nmx_up", "exp_up", "prob_up", "pT_mm", "pT_up"))
        y_mm, y_up, o_mm, h2_up, ve2_up, rstd2_up = (sem(n) for n in ("y_mm", "y_up", "o_mm", "h2_up", "ve2_up", "rstd2_up"))
        ss_up, rn_up, xn2_up, t2_mm, xnT_up, xnp_up = (sem(n) for n in ("ss_up", "rn_up", "xn2_up", "t2_mm", "xnT_up", "xnp_up"))
        phsq_up, phss_mm, phss_up, pinv_up, dsc_up, dsc_mm, phin_up = (
            sem(n) for n in ("phsq_up", "phss_mm", "phss_up", "pinv_up", "dsc_up", "dsc_mm", "phin_up"))
        lg_mm, lgm_up, lge_up, nM_up, tE_up, dw_up, gate_up, gT_mm, gT_up = (
            sem(n) for n in ("lg_mm", "lgm_up", "lge_up", "nM_up", "tE_up", "dw_up", "gate_up", "gT_mm", "gT_up"))
        link_s = sem("dve_link")
        w1_hi, w1_lo, w2_hi, w2_lo = (sem(n) for n in ("w1_hi", "w1_lo", "w2_hi", "w2_lo"))
        f1_bank, gelu_bank, h_hi, h_lo = (sem(n) for n in ("f1_bank", "gelu_bank", "h_hi", "h_lo"))
        f2_bank, eo_cp, eo_add = (sem(n) for n in ("f2_bank", "eo_cp", "eo_add"))
        cws_up, cwT_mm, cwT_up, comb = (sem(n) for n in ("cws_up", "cwT_mm", "cwT_up", "comb"))
        sl_mm, sl_hi, sl_lo = (sem(n) for n in ("sl_mm", "sl_hi", "sl_lo"))

        block = ctx.enter_context(nc.Block())

        def wait(eng, s, value):
            if not isinstance(value, int) or value > 0:
                eng.wait_ge(s, value)

        def groups(eng, body):
            body(0, True, False)
            with eng.Fori(1, NG - 1) as j:
                body(j, False, False)
            body(NG - 1, False, True)

        @block.sync
        def _(sp):
            for a in range(2):
                sp.dma_start(xTs[:, 3 * a:3 * a + 3, :], xT[:, 3 * a:3 * a + 3, :]).then_inc(tok_in, 16)
            sp.dma_start(wtk, wtokT).then_inc(tok_in, 16)
            sp.dma_start(rb[:, :, :], rowbias.partition_broadcast(P)).then_inc(bias_in, 16)
            sp.dma_start(phA[:, :], phi[0:P, :]).then_inc(phi_in, 16)
            sp.dma_start(phC[:, :], phi[P:D, :]).then_inc(phi_in, 16)
            sp.dma_start(scl[:, :], scale.partition_broadcast(P)).then_inc(phi_in, 16)
            sp.dma_start(b2s[:, :], b2).then_inc(phi_in, 16)
            sp.dma_start(wat[:, :, :], wattnAB).then_inc(attn_in, 16)
            sp.dma_start(watC[:, :, :], wattnC).then_inc(attn_in, 16)
            sp.dma_start(bqk[:, :], bqkAB).then_inc(attn_in, 16)
            sp.dma_start(bqk_c[:, :], bqkC).then_inc(attn_in, 16)

            def load(slot, e):
                sp.dma_start(rawA[:, slot, 0:H], wA[bass.ds(e, 1), :, 0:H]).then_inc(w1_in[slot], 16)
                sp.dma_start(rawC[:, slot, :], wC[bass.ds(e, 1), :, :]).then_inc(w1_in[slot], 16)
                sp.dma_start(rawA[:, slot, H:], wA[bass.ds(e, 1), :, H:]).then_inc(w2_in[slot], 16)

            for e in range(EG):
                load(e, e)

            def body(j, first, last):
                for i in range(EG):
                    e = j * EG + i
                    if not last:
                        sp.wait_ge(w1_lo, e + 1)
                        sp.wait_ge(w2_lo, e + 1)
                        sp.wait_ge(gelu_bank, e * 3 + 3)
                        load(i, e + EG)
                    for r in range(2):
                        sp.wait_ge(eo_add, e * 2 + (r + 1))
                        if i == 0 and r == 0:
                            wait(sp, comb, j)
                        for b in range(P // S):
                            sp.dma_start(eog[S * i:S * i + S, 4 * r + b, :],
                                         eot[S * b:S * b + S, r, :]).then_inc(eo_in[i], 16)

            groups(sp, body)
            for t in range(2):
                sp.wait_ge(h_up, NT + 1 + t)
                sp.dma_start(out_v[:, 2 * t:2 * t + 2, :], xn[:, 2 * t:2 * t + 2, :]).then_inc(out_done, 16)
            sp.wait_ge(out_done, 32)

        @block.gpsimd
        def _(pool):
            nc.gpsimd.memset(ident[:, :], 0.0).then_inc(id_up, 1)
            nc.gpsimd.memset(ones[:, :], 1.0).then_inc(const_up, 1)
            nc.gpsimd.memset(mhalf[:, :], -0.5).then_inc(const_up, 1)
            pool.wait_ge(id_up, 1)
            nc.gpsimd.affine_select(out=ident[:, :], in_=ident[:, :], compare_op=ALU.not_equal, fill=1.0, base=0,
                                    pattern=[[-1, P]], channel_multiplier=1).then_inc(id_up, 1)
            nc.gpsimd.memset(prob[:, :, :], 0.0).then_inc(const_up, 1)
            nc.gpsimd.memset(xnp[:, :, :], 0.0).then_inc(const_up, 1)
            pool.wait_ge(const_up, 4)
            for t in range(NT):
                pool.wait_ge(ve_up, t + 1)
                nc.gpsimd.tensor_tensor(rstd[:, t:t + 1], ve[:, t:t + 1], mhalf[:, 0:1], ALU.pow).then_inc(rstd_up, 1)
            pool.wait_ge(phss_up, 1)
            nc.gpsimd.tensor_tensor(pinv[:, :], pss[:, :], mhalf[:, :], ALU.pow).then_inc(pinv_up, 1)
            for t in range(NT):
                pool.wait_ge(ve2_up, t + 1)
                nc.gpsimd.tensor_tensor(rstd[:, t:t + 1], ve[:, t:t + 1], mhalf[:, 0:1], ALU.pow).then_inc(rstd2_up, 1)
                pool.wait_ge(ss_up, t + 1)
                nc.gpsimd.tensor_tensor(rn[:, t:t + 1], ss[:, t:t + 1], mhalf[:, 0:1], ALU.pow).then_inc(rn_up, 1)
            for b in range(B):
                lo = L * (b % 2)
                pool.wait_ge(xn2_up, b // 2 + 1)
                if b == 0:
                    pool.wait_ge(rn_up, NT)
                else:
                    pool.wait_ge(xnp_up, b)
                nc.gpsimd.tensor_copy(xnp[lo:lo + L, b, 0:D], xn[lo:lo + L, b // 2, :])
                nc.gpsimd.tensor_copy(xnp[lo:lo + L, b, D:], xn[lo:lo + L, b // 2, P:D]).then_inc(xnp_up, 1)

        @block.scalar
        def _(act):
            act.wait_ge(phi_in, 64)
            nc.scalar.activation(phsq, phA[:, :], ACT.Square)
            nc.scalar.activation(phsqC, phC[:, :], ACT.Square).then_inc(phsq_up, 1)

            def w1_split(e, par, slot, grp):
                act.wait_ge(w1_in[slot], grp * 32 + 32)
                wait(act, f1_bank, (e - 2) * 3 + 3 if not isinstance(e, int) or e >= 2 else 0)
                nc.scalar.activation(w1h[:, par, :], rawA[:, slot, 0:H], ACT.Copy)
                nc.scalar.activation(w1c[0:DC, par, :], rawC[:, slot, :], ACT.Copy).then_inc(w1_hi, 1)

            def w2_split(e, par, slot, grp):
                act.wait_ge(w2_in[slot], grp * 16 + 16)
                wait(act, f2_bank, (e - 2) * 2 + 2 if not isinstance(e, int) or e >= 2 else 0)
                nc.scalar.activation(w2s[:, par, :, 0:D],
                                     rawA[:, slot, H:H + HT * D].rearrange("p (t d) -> p t d", t=HT),
                                     ACT.Copy).then_inc(w2_hi, 1)

            def gelu(n, par, slot, grp):
                act.wait_ge(w2_in[slot], grp * 16 + 16)
                wait(act, h_lo, (n - 2) * 3 + 3 if not isinstance(n, int) or n >= 2 else 0)
                for k in range(3):
                    act.wait_ge(f1_bank, n * 3 + (k + 1))
                    for m in range(2):
                        t = 2 * k + m
                        at = par * HT * ROWS + t * ROWS
                        g = nc.scalar.activation(hf[:, at:at + ROWS], R[:, k, m * ROWS:(m + 1) * ROWS], ACT.Gelu,
                                                 bias=rawA[:, slot, H + HT * D + t:H + HT * D + t + 1])
                    g.then_inc(gelu_bank, 1)

            def slots_hi(jj):
                for q in range(4):
                    x = (xABh, xCh)[q % 2]
                    c0 = P * (q // 2)
                    act.wait_ge(sl_mm, jj * 4 + (q + 1))
                    nc.scalar.activation(
                        x[:, :, c0:c0 + P].rearrange("p e (b s) -> p b e s", s=S),
                        R[:, (G, 0, 1, 2)[q], :].rearrange("p (b e s) -> p b e s", b=4, e=EG),
                        ACT.Copy).then_inc(sl_hi, 1)

            for t in range(NT):
                c = slice(P * t, P * t + P)
                act.wait_ge(t1_mm, t + 1)
                nc.scalar.activation(xT2[:, 0, c], EO[:, t % 2, 0:P], ACT.Copy)
                nc.scalar.activation(xT2[0:DC, 1, c], EO[0:DC, t % 2, P:2 * P], ACT.Copy).then_inc(x1T_up, 1)
                if t == 0:
                    act.wait_ge(attn_in, 64)
                    act.wait_ge(phss_mm, 1)
                act.wait_ge(qk_mm, t + 1)
                nc.scalar.activation(qA[:, c], R[:, t, 0:P], ACT.Identity, bias=bqk[:, 0:1])
                nc.scalar.activation(qC[:, c], R[0:DC, t, P:2 * P], ACT.Identity, bias=bqk_c[:, 0:1])
                nc.scalar.activation(kA[:, c], R[:, t, 2 * P:3 * P], ACT.Identity, bias=bqk[:, 1:2])
                nc.scalar.activation(kC[:, c], R[0:DC, t, 3 * P:4 * P], ACT.Identity,
                                     bias=bqk_c[:, 1:2]).then_inc(qk_up, 1)
            w1_split(0, 0, 0, 0)
            for t in range(NT):
                act.wait_ge(nmx_up, t + 1)
                act.wait_ge(const_up, 4)
                for a in range(2):
                    r = slice(L * a, L * a + L)
                    x = nc.scalar.activation(prob[r, t, L * a:L * a + L], R[r, t, L * a:L * a + L], ACT.Exp,
                                             bias=nmx[r, t:t + 1], accum_out=asum[r, t:t + 1])
                x.then_inc(exp_up, 1)
            w1_split(1, 1, 1, 0)
            for t in range(NT):
                act.wait_ge(pT_mm, t + 1)
                nc.scalar.activation(probT[:, P * t:P * t + P], R[:, t, P:2 * P], ACT.Copy).then_inc(pT_up, 1)
            for t in range(NT):
                c = slice(P * t, P * t + P)
                act.wait_ge(y_mm, t + 1)
                nc.scalar.activation(yA[:, c], R[:, t, 2 * P:3 * P], ACT.Copy)
                nc.scalar.activation(yC[:, c], R[0:DC, t, 3 * P:4 * P], ACT.Copy).then_inc(y_up, 1)
            w2_split(0, 0, 0, 0)
            for t in range(NT):
                act.wait_ge(t2_mm, t + 1)
                nc.scalar.activation(xT2[:, 0, P * t:P * t + P], EO[:, t % 2, 0:P], ACT.Copy)
                nc.scalar.activation(xT2[0:DC, 1, P * t:P * t + P], EO[0:DC, t % 2, P:2 * P],
                                     ACT.Copy).then_inc(xnT_up, 1)
            for t in range(NT):
                act.wait_ge(lgm_up, t + 1)
                nc.scalar.activation(dw[:, t, :], dw[:, t, :], ACT.Exp).then_inc(lge_up, 1)
                act.wait_ge(nM_up, t + 1)
                nc.scalar.activation(tE[:, t, :], mE[:, t, :], ACT.Exp, bias=nM[:, t:t + 1]).then_inc(tE_up, 1)
            slots_hi(0)
            act.wait_ge(gT_mm, NT)
            nc.scalar.activation(gateT[:, :], EO[0:E, 0, :], ACT.Copy).then_inc(gT_up, 1)
            gelu(0, 0, 0, 0)

            def body(j, first, last):
                for i in range(EG):
                    e = j * EG + i
                    more = not (last and i == EG - 1)
                    if more:
                        gelu(e + 1, (i + 1) % 2, (i + 1) % EG, j + (i + 1) // EG)
                    if not (last and i >= EG - 2):
                        w1_split(e + 2, i % 2, (i + 2) % EG, j + (i + 2) // EG)
                    for r in range(2):
                        act.wait_ge(f2_bank, e * 2 + (r + 1))
                        wait(act, eo_add, e * 2 + (r - 1))
                        nc.scalar.activation(eol[:, r, :], EO[:, r, D:2 * D], ACT.Copy).then_inc(eo_cp, 1)
                        if r == 0:
                            if i == 1:
                                act.wait_ge(cwT_mm, j + 1)
                                wait(act, comb, j)
                                nc.scalar.activation(cwT[:, :], R[:, G, :], ACT.Copy).then_inc(cwT_up, 1)
                            if i == 2 and not last:
                                slots_hi(j + 1)
                            if more:
                                w2_split(e + 1, (i + 1) % 2, (i + 1) % EG, j + (i + 1) // EG)

            groups(act, body)

        @block.vector
        def _(dve):
            links = [0]

            def link(ins):
                links[0] += 1
                ins.then_inc(link_s, 1)
                dve.wait_ge(link_s, links[0])

            def w1_split(e, par, slot, grp):
                dve.wait_ge(w1_hi, e + 1)
                nc.vector.tensor_tensor(w1l[:, par, :], rawA[:, slot, 0:H], w1h[:, par, :].bitcast(F32), ALU.subtract)
                nc.vector.tensor_tensor(w1c[DC:P, par, :], rawC[:, slot, :], w1c[0:DC, par, :].bitcast(F32),
                                        ALU.subtract).then_inc(w1_lo, 1)

            def w2_split(e, par, slot, grp):
                dve.wait_ge(w2_hi, e + 1)
                nc.vector.tensor_tensor(w2s[:, par, :, D:2 * D],
                                        rawA[:, slot, H:H + HT * D].rearrange("p (t d) -> p t d", t=HT),
                                        w2s[:, par, :, 0:D].bitcast(F32), ALU.subtract).then_inc(w2_lo, 1)

            def h_split(n, par):
                wait(dve, f2_bank, (n - 2) * 2 + 2 if not isinstance(n, int) or n >= 2 else 0)
                for k in range(3):
                    at = par * HT * ROWS + 2 * k * ROWS
                    whole = hf[:, at:at + 2 * ROWS].rearrange("p (t r) -> p t r", t=2)
                    hi = hh[:, par, 2 * k:2 * k + 2, :]
                    dve.wait_ge(gelu_bank, n * 3 + (k + 1))
                    nc.vector.tensor_copy(hi, whole).then_inc(h_hi, 1)
                    dve.wait_ge(h_hi, n * 3 + (k + 1))
                    nc.vector.tensor_tensor(hl[:, par, 2 * k:2 * k + 2, :], whole, hi.bitcast(F32),
                                            ALU.subtract).then_inc(h_lo, 1)

            def slots_lo(jj):
                for q in range(4):
                    hi, lo = ((xABh, xABl), (xCh, xCl))[q % 2]
                    c0 = P * (q // 2)
                    dve.wait_ge(sl_hi, jj * 4 + (q + 1))
                    view = "p e (b s) -> p b e s"
                    nc.vector.tensor_tensor(
                        lo[:, :, c0:c0 + P].rearrange(view, s=S),
                        R[:, (G, 0, 1, 2)[q], :].rearrange("p (b e s) -> p b e s", b=4, e=EG),
                        hi[:, :, c0:c0 + P].rearrange(view, s=S).bitcast(F32), ALU.subtract).then_inc(sl_lo, 1)

            def stats(t, up):
                link(nc.vector.bn_stats(st[:, t, :], h[:, t, :]))
                link(nc.vector.bn_aggr(mv[:, t, :], st[:, t, :]))
                nc.vector.tensor_scalar(ve[:, t:t + 1], mv[:, t, 1:2], LN_EPS, None, ALU.add).then_inc(up, 1)

            dve.wait_ge(bias_in, 16)
            for t in range(NT):
                dve.wait_ge(tok_mm, t + 1)
                link(nc.vector.tensor_tensor(h[:, t, :], R[:, t, 0:D], rb[:, 0, :], ALU.add))
                stats(t, ve_up)
            for t in range(NT):
                dve.wait_ge(rstd_up, t + 1)
                nc.vector.tensor_scalar(xn[:, t, :], h[:, t, :], mv[:, t, 0:1], rstd[:, t:t + 1], ALU.subtract,
                                        ALU.mult).then_inc(xn1_up, 1)
            dve.wait_ge(phss_mm, 1)
            nc.vector.tensor_scalar(pss[:, :], Y[:, 0, 0:E * S // P], L2_EPS2, None, ALU.max).then_inc(phss_up, 1)
            dve.wait_ge(xn1_up, NT)
            for t in range(NT):
                nc.vector.tensor_tensor(h[:, t, :], h[:, t, :], rb[:, 2, :], ALU.add).then_inc(h_up, 1)
            dve.wait_ge(pinv_up, 1)
            dve.wait_ge(id_up, 2)
            dve.wait_ge(phi_in, 64)
            for c in range(E * S // P):
                if c >= 2:
                    dve.wait_ge(dsc_mm, c - 1)
                nc.vector.tensor_scalar(dsc[:, c % 2, :], ident[:, :], pinv[:, c:c + 1], scl[:, 0:1], ALU.mult,
                                        ALU.mult).then_inc(dsc_up, 1)
            dve.wait_ge(dsc_mm, E * S // P)
            flat = Y[:, :, :].rearrange("p a n -> p (a n)")
            dve.wait_ge(phsq_up, 1)
            nc.vector.tensor_tensor(phA[:, :], flat, phA[:, :], ALU.mult)
            nc.vector.tensor_tensor(phC[:, :], flat[0:DC, :], phC[:, :], ALU.mult).then_inc(phin_up, 1)
            for t in range(NT):
                dve.wait_ge(v_mm, t + 1)
                nc.vector.tensor_tensor(v[:, t, :], EO[:, t % 2, 2 * P:2 * P + D], rb[:, 1, :],
                                        ALU.add).then_inc(v_up, 1)
            w1_split(0, 0, 0, 0)
            for t in range(NT):
                dve.wait_ge(sc_mm, t + 1)
                for a in range(2):
                    r = slice(L * a, L * a + L)
                    x = nc.vector.tensor_reduce(nmx[r, t:t + 1], R[r, t, L * a:L * a + L], AX.X, ALU.max, negate=True)
                x.then_inc(nmx_up, 1)
            for t in range(NT):
                dve.wait_ge(exp_up, t + 1)
                link(nc.vector.reciprocal(arec[:, t:t + 1], asum[:, t:t + 1]))
                nc.vector.tensor_scalar(prob[:, t, :], prob[:, t, :], arec[:, t:t + 1], None,
                                        ALU.mult).then_inc(prob_up, 1)
            w1_split(1, 1, 1, 0)
            for t in range(NT):
                dve.wait_ge(o_mm, t + 1)
                if t == 0:
                    dve.wait_ge(h_up, NT)
                link(nc.vector.tensor_tensor(h[:, t, :], EO[:, t % 2, 2 * P:2 * P + D], h[:, t, :], ALU.add))
                h2 = stats(t, ve2_up)
            for t in range(NT):
                dve.wait_ge(rstd2_up, t + 1)
                link(nc.vector.tensor_scalar(xn[:, t, :], h[:, t, :], mv[:, t, 0:1], rstd[:, t:t + 1], ALU.subtract,
                                             ALU.mult))
                link(nc.vector.tensor_tensor_reduce(out=sq[:, t, :], in0=xn[:, t, :], in1=xn[:, t, :], scale=1.0,
                                                    scalar=0.0, op0=ALU.mult, op1=ALU.add, accum_out=ss[:, t:t + 1]))
                nc.vector.tensor_scalar(ss[:, t:t + 1], ss[:, t:t + 1], L2_EPS2, None, ALU.max).then_inc(ss_up, 1)
                dve.wait_ge(rn_up, t + 1)
                nc.vector.tensor_scalar(xn[:, t, :], xn[:, t, :], rn[:, t:t + 1], None, ALU.mult).then_inc(xn2_up, 1)
            w2_split(0, 0, 0, 0)

            def bc(x):
                return x.unsqueeze(2).broadcast_to([P, E, S])

            def less_max(t):
                a = 2 * (t % 2)
                lg = R[:, a:a + 2, :].rearrange("p a (e s) -> p (a e) s", s=S)
                dve.wait_ge(lg_mm, t + 1)
                link(nc.vector.tensor_reduce(mE[:, t, :], lg, AX.X, ALU.max))
                nc.vector.tensor_tensor(dw[:, t, :].rearrange("p (e s) -> p e s", s=S), lg, bc(mE[:, t, :]),
                                        ALU.subtract).then_inc(lgm_up, 1)
                nc.vector.tensor_reduce(nM[:, t:t + 1], mE[:, t, :], AX.X, ALU.max, negate=True).then_inc(nM_up, 1)

            def weights(t):
                d3 = dw[:, t, :].rearrange("p (e s) -> p e s", s=S)
                dve.wait_ge(lge_up, t + 1)
                link(nc.vector.tensor_reduce(sE[:, t, :], d3, AX.X, ALU.add))
                link(nc.vector.reciprocal(rE[:, t, :], sE[:, t, :]))
                nc.vector.tensor_tensor(d3, d3, bc(rE[:, t, :]), ALU.mult).then_inc(dw_up, 1)
                dve.wait_ge(tE_up, t + 1)
                link(nc.vector.tensor_tensor(uE[:, t, :], sE[:, t, :], tE[:, t, :], ALU.mult))
                link(nc.vector.tensor_reduce(uS[:, t:t + 1], uE[:, t, :], AX.X, ALU.add))
                link(nc.vector.reciprocal(ru[:, t:t + 1], uS[:, t:t + 1]))
                nc.vector.tensor_scalar(gate[:, t, :], uE[:, t, :], ru[:, t:t + 1], None, ALU.mult).then_inc(gate_up, 1)

            less_max(0)
            for t in range(NT):
                if t + 1 < NT:
                    less_max(t + 1)
                weights(t)
            slots_lo(0)
            h_split(0, 0)
            dve.wait_ge(gate_up, NT)
            dve.wait_ge(dw_up, NT)

            def body(j, first, last):
                for i in range(EG):
                    e = j * EG + i
                    more = not (last and i == EG - 1)
                    if more:
                        h_split(e + 1, (i + 1) % 2)
                    if not (last and i >= EG - 2):
                        w1_split(e + 2, i % 2, (i + 2) % EG, j + (i + 2) // EG)
                    if i == 1:
                        wait(dve, cwT_mm, j)
                        for t in range(NT):
                            x = nc.vector.tensor_tensor(
                                cws[:, t, :].rearrange("p (e s) -> p e s", s=S),
                                dw[:, t, bass.ds(j * GC, GC)].rearrange("p (e s) -> p e s", s=S),
                                gate[:, t, bass.ds(j * EG, EG)].unsqueeze(2).broadcast_to([P, EG, S]), ALU.mult)
                        x.then_inc(cws_up, 1)
                    for r in range(2):
                        dve.wait_ge(eo_cp, e * 2 + (r + 1))
                        if not (first and i == 0):
                            dve.wait_ge(eo_in[(i - 1) % EG], (j + 1 if i else j) * EO_IN)
                        nc.vector.tensor_tensor(eot[:, r, :], EO[:, r, 0:D], eol[:, r, :], ALU.add).then_inc(eo_add, 1)
                        if r == 0:
                            if i == 2 and not last:
                                slots_lo(j + 1)
                            if more:
                                w2_split(e + 1, (i + 1) % 2, (i + 1) % EG, j + (i + 1) // EG)

            groups(dve, body)
            dve.wait_ge(comb, NG)
            for t in range(2):
                nc.vector.tensor_tensor(xn[:, 2 * t:2 * t + 2, :],
                                        Y[:, t, 0:2 * D].rearrange("p (a d) -> p a d", a=2),
                                        h[:, 2 * t:2 * t + 2, :], ALU.add).then_inc(h_up, 1)

        @block.tensor
        def _(pe):
            mm = nc.tensor.matmul

            pe.wait_ge(tok_in, 48)
            for t in range(NT):
                for k in range(PK):
                    x = mm(R[:, t, 0:D], xTs[:, k, P * t:P * t + P], wtk[:, k, :], start=(k == 0), stop=(k == PK - 1))
                x.then_inc(tok_mm, 1)
            pe.wait_ge(phsq_up, 1)
            pe.wait_ge(const_up, 4)
            for c in range(E * S // P):
                mm(Y[:, 0, c:c + 1], phsq[:, P * c:P * c + P], ones[:, 0:1], start=True, stop=False)
                x = mm(Y[:, 0, c:c + 1], phsqC[:, P * c:P * c + P], ones[0:DC, 0:1], start=False, stop=True)
            x.then_inc(phss_mm, 1)

            def transposes(t, src, done):
                nc.tensor.transpose(EO[:, t % 2, 0:P], src[:, t, 0:P], ident[:, :])
                nc.tensor.transpose(EO[0:DC, t % 2, P:2 * P], src[:, t, P:D], ident[:, :]).then_inc(done, 1)

            pe.wait_ge(id_up, 2)
            pe.wait_ge(attn_in, 64)
            for t in range(NT):
                c = slice(P * t, P * t + P)
                pe.wait_ge(xn1_up, t + 1)
                wait(pe, v_up, t - 1)
                transposes(t, xn, t1_mm)
                pe.wait_ge(x1T_up, t + 1)
                for w in range(2):
                    at = 2 * P * w
                    mm(R[:, t, at:at + P], wat[:, w, 0:P], xT2[:, 0, c], start=True, stop=False)
                    mm(R[:, t, at:at + P], watC[:, w, 0:P], xT2[0:DC, 1, c], start=False, stop=True)
                    mm(R[0:DC, t, at + P:at + 2 * P], wat[:, w, P:D], xT2[:, 0, c], start=True, stop=False)
                    x = mm(R[0:DC, t, at + P:at + 2 * P], watC[:, w, P:D], xT2[0:DC, 1, c], start=False, stop=True)
                x.then_inc(qk_mm, 1)
                mm(EO[:, t % 2, 2 * P:2 * P + D], xT2[:, 0, c], wat[:, 2, :], start=True, stop=False)
                mm(EO[:, t % 2, 2 * P:2 * P + D], xT2[0:DC, 1, c], watC[:, 2, :], start=False, stop=True).then_inc(v_mm, 1)
                if t == 1:
                    pe.wait_ge(phss_up, 1)
                    for c8 in range(E * S // P):
                        pe.wait_ge(dsc_up, c8 + 1)
                        mm(Y[:, c8 // 4, P * (c8 % 4):P * (c8 % 4) + P], ones[:, :], dsc[:, c8 % 2, :],
                           start=True, stop=True).then_inc(dsc_mm, 1)
            for t in range(NT):
                c = slice(P * t, P * t + P)
                pe.wait_ge(qk_up, t + 1)
                mm(R[:, t, 0:P], qA[:, c], kA[:, c], start=True, stop=False)
                mm(R[:, t, 0:P], qC[:, c], kC[:, c], start=False, stop=True).then_inc(sc_mm, 1)
            for t in range(NT):
                pe.wait_ge(prob_up, t + 1)
                nc.tensor.transpose(R[:, t, P:2 * P], prob[:, t, :], ident[:, :]).then_inc(pT_mm, 1)
            for t in range(NT):
                c = slice(P * t, P * t + P)
                pe.wait_ge(pT_up, t + 1)
                pe.wait_ge(v_up, t + 1)
                mm(R[:, t, 2 * P:3 * P], v[:, t, 0:P], probT[:, c], start=True, stop=True)
                mm(R[0:DC, t, 3 * P:4 * P], v[:, t, P:D], probT[:, c], start=True, stop=True).then_inc(y_mm, 1)
            for t in range(NT):
                c = slice(P * t, P * t + P)
                pe.wait_ge(y_up, t + 1)
                wait(pe, ve2_up, t - 1)
                if t < 2:
                    pe.wait_ge(v_up, NT)
                mm(EO[:, t % 2, 2 * P:2 * P + D], yA[:, c], wat[:, 3, :], start=True, stop=False)
                mm(EO[:, t % 2, 2 * P:2 * P + D], yC[:, c], watC[:, 3, :], start=False, stop=True).then_inc(o_mm, 1)
            pe.wait_ge(phin_up, 1)
            for t in range(NT):
                c = slice(P * t, P * t + P)
                pe.wait_ge(xn2_up, t + 1)
                wait(pe, xnT_up, t - 1)
                if t == 0:
                    pe.wait_ge(ve2_up, NT)
                transposes(t, xn, t2_mm)
                pe.wait_ge(xnT_up, t + 1)
                wait(pe, lgm_up, t - 1)
                for a in range(2):
                    bank = R[:, 2 * (t % 2) + a, :]
                    mm(bank, xT2[:, 0, c], phA[:, 512 * a:512 * a + 512], start=True, stop=False)
                    x = mm(bank, xT2[0:DC, 1, c], phC[:, 512 * a:512 * a + 512], start=False, stop=True)
                x.then_inc(lg_mm, 1)

            def slots(jj):
                for q in range(4):
                    part = (slice(0, P), slice(P, 2 * P))[q % 2]
                    if q == 0:
                        wait(pe, cwT_up, jj)
                    else:
                        wait(pe, gelu_bank, jj * 12 + (q - 3))
                    for b in range(4):
                        bi = 4 * (q // 2) + b
                        x = mm(R[:, (G, 0, 1, 2)[q], GC * b:GC * b + GC], xnp[:, bi, part],
                               dw[:, bi // 2, bass.ds(jj * GC, GC)], start=True, stop=True)
                    x.then_inc(sl_mm, 1)

            def f1(n, par, slot):
                pe.wait_ge(w1_lo, n + 1)
                for k in range(3):
                    wait(pe, gelu_bank, (n - 1) * 3 + (k + 1) if not isinstance(n, int) or n >= 1 else 0)
                    for m in range(2):
                        t = 2 * k + m
                        c = slice(P * t, P * t + P)
                        o = R[:, k, m * ROWS:(m + 1) * ROWS]
                        mm(o, w1h[:, par, c], xABh[:, slot, :], start=True, stop=False)
                        mm(o, w1h[:, par, c], xABl[:, slot, :], start=False, stop=False)
                        mm(o, w1l[:, par, c], xABh[:, slot, :], start=False, stop=False)
                        mm(o, w1c[:, par, c], xCh[:, slot, :], start=False, stop=False)
                        x = mm(o, w1c[:, par, c], xCl[:, slot, :], start=False, stop=True)
                    x.then_inc(f1_bank, 1)

            def f2(e, par, r):
                if r == 0:
                    pe.wait_ge(h_lo, e * 3 + 3)
                    pe.wait_ge(w2_lo, e + 1)
                wait(pe, eo_add, e * 2 + (r - 1))
                for t in range(HT):
                    rows = slice(P * r, P * r + P)
                    mm(EO[:, r, 0:2 * D], hh[:, par, t, rows], w2s[:, par, t, :], start=(t == 0), stop=False)
                    x = mm(EO[:, r, 0:D], hl[:, par, t, rows], w2s[:, par, t, 0:D], start=False, stop=(t == HT - 1))
                x.then_inc(f2_bank, 1)

            def combine(j, last):
                for i in range(EG):
                    pe.wait_ge(eo_in[i], j * EO_IN + EO_IN)
                pe.wait_ge(cwT_up, j + 1)
                for b in range(B):
                    half, at = L * (b % 2), D * ((b // 2) % 2)
                    x = mm(Y[half:half + L, b // 4, at:at + D], cwT[:, L * b:L * b + L], eog[:, b, :],
                           start=False, stop=last, skip_group_check=True)
                x.then_inc(comb, 1)

            pe.wait_ge(xnp_up, B)
            pe.wait_ge(dw_up, NT)
            slots(0)
            pe.wait_ge(gate_up, NT)
            pe.wait_ge(xnT_up, NT)
            for t in range(NT):
                nc.tensor.transpose(EO[0:E, 0, P * t:P * t + P], gate[:, t, :], ident[:, :]).then_inc(gT_mm, 1)
            pe.wait_ge(sl_lo, 4)
            f1(0, 0, 0)
            pe.wait_ge(gT_up, 1)
            for t in range(NT):
                mm(Y[:, t // 2, D * (t % 2):D * (t % 2) + D], gateT[:, P * t:P * t + P], b2s[:, :],
                   start=(t % 2 == 0), stop=False, skip_group_check=True)

            def body(j, first, last):
                for i in range(EG):
                    e = j * EG + i
                    if not (last and i == EG - 1):
                        if i == EG - 1:
                            pe.wait_ge(sl_lo, j * 4 + 8)
                        f1(e + 1, (i + 1) % 2, (i + 1) % EG)
                    f2(e, i % 2, 0)
                    if i == 0 and not first:
                        combine(j - 1, False)
                    if i == 1:
                        pe.wait_ge(cws_up, j + 1)
                        pe.wait_ge(sl_lo, j * 4 + 4)
                        for t in range(NT):
                            x = nc.tensor.transpose(R[:, G, P * t:P * t + P], cws[:, t, :], ident[:, :])
                        x.then_inc(cwT_mm, 1)
                    if i == 2 and not last:
                        slots(j + 1)
                    f2(e, i % 2, 1)

            groups(pe, body)
            combine(NG - 1, True)


_INS = ["xT", "wtokT", "rowbias", "wattnAB", "wattnC", "bqkAB", "bqkC", "phi", "scale", "b2", "wA", "wC"]


def kernel(**inputs):
    import numpy as np
    import concourse.bacc as bacc
    from concourse.bass_utils import run_bass_kernel_spmd

    def t(name):
        return np.asarray(inputs[name])

    x = t("x").reshape(B, 3, L, 2, P).transpose(4, 1, 3, 0, 2).reshape(P, PK, B * L)
    wtok = t("L0_tok_W").T.reshape(PK, P, D).transpose(1, 0, 2)
    attn = np.stack([t(f"L0_attn_w{c}").T for c in "qkvo"], axis=1)
    bqk = np.stack([t("L0_attn_bq"), t("L0_attn_bk")], axis=1)
    w1, b1, w2 = t("L0_ffn_w1"), t("L0_ffn_b1"), t("L0_ffn_w2")
    w2p = w2.reshape(E, HT, P, D).transpose(0, 2, 1, 3).reshape(E, P, HT * D)
    b1p = b1.reshape(E, HT, P).transpose(0, 2, 1)
    arrays = {
        "xT": x,
        "wtokT": wtok,
        "rowbias": np.stack([t("L0_tok_b"), t("L0_attn_bv"), t("L0_attn_bo")]),
        "wattnAB": attn[:P],
        "wattnC": attn[P:],
        "bqkAB": bqk[:P],
        "bqkC": bqk[P:],
        "phi": t("L0_ffn_phi").reshape(D, E * S),
        "scale": t("L0_ffn_scale"),
        "b2": t("L0_ffn_b2"),
        "wA": np.concatenate([w1[:, :P, :], w2p, b1p], axis=2),
        "wC": w1[:, P:, :],
    }
    arrays = {k: np.ascontiguousarray(a) for k, a in arrays.items()}
    nc = bacc.Bacc("TRN2", target_bir_lowering=False, num_devices=1)
    args = [nc.dram_tensor(f"{k}_dram", arrays[k].shape, mybir.dt.from_np(arrays[k].dtype), kind="ExternalInput").ap()
            for k in _INS]
    args.append(nc.dram_tensor("out_dram", (B, L, D), F32, kind="ExternalOutput").ap())
    vit_block(nc, *args)
    r = run_bass_kernel_spmd(nc, [{f"{k}_dram": arrays[k] for k in _INS}], core_ids=[0])
    return r.results[0]["out_dram"]
```

```python
import concourse.bass as bass
from concourse import mybir
from contextlib import ExitStack

F32 = mybir.dt.float32
F32R = mybir.dt.float32r
ALU = mybir.AluOpType
ACT = mybir.ActivationFunctionType
AX = mybir.AxisListType

P = 128
B, L, D = 8, 64, 192
DC = D - P
NT = B * L // P
PK = 6
E, S, H = 32, 32, 768
HT = H // P
ROWS = S * B
EG = 4
NG = E // EG
GC = EG * S
EO_IN = 2 * 16
LN_EPS = 1e-5
L2_EPS2 = 1e-24
SB = S // 2


def vit_block(nc, xT, wtokT, rowbias, wattnAB, wattnC, bqkAB, bqkC, phi, scale, b2, wA, wC, out):
    out_v = out.rearrange("b l d -> (b l) d").rearrange("(t p) d -> p t d", p=P)

    ctx = ExitStack()
    with ctx:
        def sb(name, shape, dt=F32):
            return ctx.enter_context(nc.sbuf_tensor(name, shape, dt))

        def sem(name):
            return ctx.enter_context(nc.semaphore(name))

        rawA = sb("rawA", [P, EG, H + HT * D + HT])
        rawC = sb("rawC", [DC, EG, H])
        w1h = sb("w1h", [P, 2, H], F32R)
        w1l = sb("w1l", [P, 2, H], F32R)
        w1c = sb("w1c", [P, 2, H], F32R)
        w2s = sb("w2s", [P, 2, HT, 2 * D], F32R)
        xABh = sb("xABh", [P, EG, ROWS], F32R)
        xABl = sb("xABl", [P, EG, ROWS], F32R)
        xCh = sb("xCh", [P, EG, ROWS], F32R)
        xCl = sb("xCl", [P, EG, ROWS], F32R)
        hf = sb("hf", [P, 2 * HT * ROWS])
        hh = sb("hh", [P, 2, HT, ROWS], F32R)
        hl = sb("hl", [P, 2, HT, ROWS], F32R)
        eol = sb("eol", [P, 2, D])
        eot = sb("eot", [P, 2, D])
        eog = sb("eog", [P, B, D])
        cws = sb("cws", [P, NT, GC])
        cwT = sb("cwT", [P, NT * P])
        dwn = sb("dwn", [P, NT, GC])
        pe_exp = sb("pe_exp", [P, NT, E * S])
        gate = sb("gate", [P, NT, E])
        gexp = sb("gexp", [P, NT, E])
        gateT = sb("gateT", [E, NT * P])
        xnp = sb("xnp", [P, B, D + DC])
        ident = sb("ident", [P, P])
        ones = sb("ones", [P, P])
        mhalf = sb("mhalf", [P, E * S // P])
        h = sb("h", [P, NT, D])
        xn = sb("xn", [P, NT, D])
        xT2 = sb("xT2", [P, 2, NT * P])
        v = sb("v", [P, NT, D])
        rb = sb("rb", [P, 3, D])
        wat = sb("wat", [P, 4, D])
        watC = sb("watC", [DC, 4, D])
        bqk = sb("bqk", [P, 2])
        bqk_c = sb("bqk_c", [DC, 2])
        phA = sb("phA", [P, E * S])
        phC = sb("phC", [DC, E * S])
        scl = sb("scl", [P, 1])
        b2s = sb("b2s", [E, D])
        st = sb("st", [P, NT, 6])
        mv = sb("mv", [P, NT, 2])
        ve = sb("ve", [P, NT])
        rstd = sb("rstd", [P, NT])
        rve = sb("rve", [P, NT])
        pw = sb("pw", [P, NT, 2])
        pwr = sb("pwr", [P, NT, 2])
        f2n = sb("f2n", [P, NT])
        pss = sb("pss", [P, E * S // P])
        pinv = sb("pinv", [P, E * S // P])
        nmx = sb("nmx", [P, NT])
        asum = sb("asum", [P, NT])
        arec = sb("arec", [P, NT])
        mE = sb("mE", [P, NT, E])
        nM = sb("nM", [P, NT])
        tE = sb("tE", [P, NT, E])
        sE = sb("sE", [P, NT, E])
        rE = sb("rE", [P, NT, E])
        uE = sb("uE", [P, NT, E])
        uS = sb("uS", [P, NT])
        ru = sb("ru", [P, NT])

        xTs = pe_exp[:, 0:3, :].rearrange("p a n -> p (a n)").rearrange("p (k t) -> p k t", k=PK)
        phsq = pe_exp[:, 3, :]
        wtk = eog[:, 0:PK, :]
        qA, kA = hf[:, 0:512], hf[:, 512:1024]
        qC, kC = hf[0:DC, 1024:1536], hf[0:DC, 1536:2048]
        yA, yC = hf[:, 2048:2560], hf[0:DC, 2560:3072]
        phsqC = hf[0:DC, 2048:3072]
        dsc = phsq.rearrange("p (c n) -> p c n", n=P)
        prob = cws
        probT = cwT

        R = ctx.enter_context(nc.psum_tensor("R", [P, 4, 512], F32))
        EO = ctx.enter_context(nc.psum_tensor("EO", [P, 2, 512], F32))
        Y = ctx.enter_context(nc.psum_tensor("Y", [P, 2, 512], F32))
        G = 3

        tok_in, bias_in, attn_in, phi_in, b2_in = (sem(n) for n in ("tok_in", "bias_in", "attn_in", "phi_in", "b2_in"))
        w1_in = [sem(f"w1_in{s}") for s in range(EG)]
        w2_in = [sem(f"w2_in{s}") for s in range(EG)]
        eo_in = [sem(f"eo_in{s}") for s in range(EG)]
        out_done = sem("out_done")
        const_up, id_up = sem("const_up"), sem("id_up")
        tok_mm, ve_up, rstd_up, xn1_up = (sem(n) for n in ("tok_mm", "ve_up", "rstd_up", "xn1_up"))
        t1_mm, x1T_up, qk_mm, v_mm, qk_up, v_up = (sem(n) for n in ("t1_mm", "x1T_up", "qk_mm", "v_mm", "qk_up", "v_up"))
        sc_mm, nmx_up, exp_up, prob_up, pT_mm, pT_up = (sem(n) for n in ("sc_mm", "nmx_up", "exp_up", "prob_up", "pT_mm", "pT_up"))
        y_mm, y_up, o_mm, h2_up, pw_up, pwr_up = (sem(n) for n in ("y_mm", "y_up", "o_mm", "h2_up", "pw_up", "pwr_up"))
        hb_up, xn2_up, t2_mm, xnT_up, xnp_up, fin_up = (sem(n) for n in ("hb_up", "xn2_up", "t2_mm", "xnT_up", "xnp_up", "fin_up"))
        phsq_up, phss_mm, phss_up, pinv_up, dsc_up, dsc_mm, phin_up = (
            sem(n) for n in ("phsq_up", "phss_mm", "phss_up", "pinv_up", "dsc_up", "dsc_mm", "phin_up"))
        lg_mm, lgm_up, lge_up, nM_up, tE_up, rE_up, gate_up, gT_mm, gT_up = (
            sem(n) for n in ("lg_mm", "lgm_up", "lge_up", "nM_up", "tE_up", "rE_up", "gate_up", "gT_mm", "gT_up"))
        link_s = sem("dve_link")
        w1_hi, w1_lo, w2_hi, w2_lo = (sem(n) for n in ("w1_hi", "w1_lo", "w2_hi", "w2_lo"))
        f1_bank, gelu_bank, h_hi, h_hi1, h_lo = (sem(n) for n in ("f1_bank", "gelu_bank", "h_hi", "h_hi1", "h_lo"))
        f2_bank, eo_cp, eo_add = (sem(n) for n in ("f2_bank", "eo_cp", "eo_add"))
        cws_up, cwT_mm, cwT_up, comb = (sem(n) for n in ("cws_up", "cwT_mm", "cwT_up", "comb"))
        dwn_up = sem("dwn_up")
        sl_mm, sl_hi, sl_lo = (sem(n) for n in ("sl_mm", "sl_hi", "sl_lo"))

        block = ctx.enter_context(nc.Block())

        def wait(eng, s, value):
            if not isinstance(value, int) or value > 0:
                eng.wait_ge(s, value)

        def groups(eng, body):
            body(0, True, False)
            with eng.Fori(1, NG - 1) as j:
                body(j, False, False)
            body(NG - 1, False, True)

        def load(slot, e):
            nc.sync.dma_start(rawA[:, slot, 0:H], wA[bass.ds(e, 1), :, 0:H]).then_inc(w1_in[slot], 16)
            nc.sync.dma_start(rawC[:, slot, :], wC[bass.ds(e, 1), :, :]).then_inc(w1_in[slot], 16)
            nc.sync.dma_start(rawA[:, slot, H:], wA[bass.ds(e, 1), :, H:]).then_inc(w2_in[slot], 16)

        def hidden(par, k):
            at = (par * HT + 2 * k) * ROWS
            return hf[:, at:at + 2 * ROWS].rearrange("p (t r) -> p t r", t=2)

        def slot_bank(q):
            return R[:, (G, 0, 1, 2)[q], :].rearrange("p (b n) -> p n b", b=4)

        def images(x, half):
            return x[:, :, :].rearrange("p e (s b) -> p (e s) b", b=B)[:, :, 4 * half:4 * half + 4]

        def logit_banks(t):
            return Y[:, :, :] if t % 2 == 0 else R[:, t - 1:t + 1, :]

        def wave(*stages):
            for step in range(NT + max(lag for _, lag in stages)):
                for stage, lag in stages:
                    if 0 <= step - lag < NT:
                        stage(step - lag)

        @block.sync
        def _(sp):
            sp.dma_start(phA[:, :], phi[0:P, :]).then_inc(phi_in, 16)
            sp.dma_start(phC[:, :], phi[P:D, :]).then_inc(phi_in, 16)
            sp.dma_start(wtk, wtokT).then_inc(tok_in, 16)
            for a in range(2):
                sp.dma_start(xTs[:, 3 * a:3 * a + 3, :], xT[:, 3 * a:3 * a + 3, :]).then_inc(tok_in, 16)
            sp.dma_start(rb[:, :, :], rowbias.partition_broadcast(P)).then_inc(bias_in, 16)
            sp.dma_start(scl[:, :], scale.partition_broadcast(P)).then_inc(bias_in, 16)
            sp.dma_start(wat[:, :, :], wattnAB).then_inc(attn_in, 16)
            sp.dma_start(watC[:, :, :], wattnC).then_inc(attn_in, 16)
            sp.dma_start(bqk[:, :], bqkAB).then_inc(attn_in, 16)
            sp.dma_start(bqk_c[:, :], bqkC).then_inc(attn_in, 16)
            for e in range(EG):
                load(e, e)
            sp.dma_start(b2s[:, :], b2).then_inc(b2_in, 16)

            def body(j, first, last):
                for i in range(EG):
                    e = j * EG + i
                    for r in range(2):
                        sp.wait_ge(eo_add, e * 2 + (r + 1))
                        if i == 0 and r == 0:
                            wait(sp, comb, j)
                        at = S * i + SB * r
                        sp.dma_start(eog[at:at + SB, :, :], eot[:, r, :]).then_inc(eo_in[i], 16)
                    if not last:
                        sp.wait_ge(w1_lo, e + 1)
                        sp.wait_ge(w2_lo, e + 1)
                        sp.wait_ge(gelu_bank, e * 3 + 3)
                        load(i, e + EG)

            groups(sp, body)
            for t in range(2):
                sp.wait_ge(fin_up, t + 1)
                sp.dma_start(out_v[:, 2 * t:2 * t + 2, :], xn[:, 2 * t:2 * t + 2, :]).then_inc(out_done, 16)
            sp.wait_ge(out_done, 32)

        @block.gpsimd
        def _(pool):
            nc.gpsimd.memset(ident[:, :], 0.0).then_inc(id_up, 1)
            nc.gpsimd.memset(ones[:, :], 1.0).then_inc(const_up, 1)
            nc.gpsimd.memset(mhalf[:, :], -0.5).then_inc(const_up, 1)
            pool.wait_ge(id_up, 1)
            nc.gpsimd.affine_select(out=ident[:, :], in_=ident[:, :], compare_op=ALU.not_equal, fill=1.0, base=0,
                                    pattern=[[-1, P]], channel_multiplier=1).then_inc(id_up, 1)
            nc.gpsimd.memset(prob[:, :, :], 0.0).then_inc(const_up, 1)
            nc.gpsimd.memset(xnp[:, :, :], 0.0).then_inc(const_up, 1)
            pool.wait_ge(const_up, 4)
            pool.wait_ge(phss_up, 1)
            nc.gpsimd.tensor_tensor(pinv[:, :], pss[:, :], mhalf[:, :], ALU.pow).then_inc(pinv_up, 1)

            def pow1(t):
                pool.wait_ge(ve_up, t + 1)
                nc.gpsimd.tensor_tensor(rstd[:, t:t + 1], ve[:, t:t + 1], mhalf[:, 0:1], ALU.pow).then_inc(rstd_up, 1)

            def pow2(t):
                pool.wait_ge(pw_up, t + 1)
                nc.gpsimd.tensor_tensor(pwr[:, t, :], pw[:, t, :], mhalf[:, 0:2], ALU.pow).then_inc(pwr_up, 1)

            def spread(t):
                pool.wait_ge(xn2_up, t + 1)
                for a in range(2):
                    r = slice(L * a, L * a + L)
                    if a:
                        pool.wait_ge(xnp_up, 2 * t + a)
                    else:
                        pool.wait_ge(pwr_up, min(t + 2, NT))
                    nc.gpsimd.tensor_copy(xnp[r, 2 * t + a, 0:D], xn[r, t, :])
                    nc.gpsimd.tensor_copy(xnp[r, 2 * t + a, D:], xn[r, t, P:D]).then_inc(xnp_up, 1)
                pool.wait_ge(xnp_up, 2 * t + 2)

            wave((pow1, 0), (pow2, 3), (spread, 4))

            def experts_of(x, j, t):
                return x[:, t, bass.ds(j * EG, EG)].unsqueeze(2).broadcast_to([P, EG, S])

            def weights(dst, j, t, scales):
                return nc.gpsimd.tensor_tensor(
                    dst[:, t, :].rearrange("p (e s) -> p e s", s=S),
                    pe_exp[:, t, bass.ds(j * GC, GC)].rearrange("p (e s) -> p e s", s=S),
                    experts_of(scales, j, t), ALU.mult)

            for t in range(NT):
                pool.wait_ge(rE_up, t + 1)
                weights(dwn, 0, t, rE).then_inc(dwn_up, 1)
            pool.wait_ge(gate_up, 1)

            def body(j, first, last):
                for i in range(2):
                    if i == 0:
                        wait(pool, cwT_mm, j)
                        for t in range(NT):
                            x = weights(cws, j, t, gexp)
                        x.then_inc(cws_up, 1)
                    if i == 1 and not last:
                        pool.wait_ge(sl_mm, j * 4 + 4)
                        for t in range(NT):
                            weights(dwn, j + 1, t, rE).then_inc(dwn_up, 1)

            groups(pool, body)

        @block.scalar
        def _(act):
            act.wait_ge(phi_in, 32)
            nc.scalar.activation(phsq, phA[:, :], ACT.Square)
            nc.scalar.activation(phsqC, phC[:, :], ACT.Square).then_inc(phsq_up, 1)

            def w1_split(e, par, slot, grp):
                act.wait_ge(w1_in[slot], grp * 32 + 32)
                wait(act, f1_bank, (e - 2) * 3 + 3 if not isinstance(e, int) or e >= 2 else 0)
                nc.scalar.activation(w1h[:, par, :], rawA[:, slot, 0:H], ACT.Copy).then_inc(w1_hi, 1)
                nc.scalar.activation(w1c[0:DC, par, :], rawC[:, slot, :], ACT.Copy).then_inc(w1_hi, 1)

            def w2_split(e, par, slot, grp):
                act.wait_ge(w2_in[slot], grp * 16 + 16)
                wait(act, f2_bank, (e - 2) * 2 + 2 if not isinstance(e, int) or e >= 2 else 0)
                nc.scalar.activation(w2s[:, par, :, 0:D],
                                     rawA[:, slot, H:H + HT * D].rearrange("p (t d) -> p t d", t=HT),
                                     ACT.Copy).then_inc(w2_hi, 1)

            def gelu(n, par, slot, grp):
                act.wait_ge(w2_in[slot], grp * 16 + 16)
                wait(act, h_lo, (n - 2) * 3 + 3 if not isinstance(n, int) or n >= 2 else 0)
                for k in range(3):
                    act.wait_ge(f1_bank, n * 3 + (k + 1))
                    for m in range(2):
                        t = 2 * k + m
                        at = par * HT * ROWS + t * ROWS
                        g = nc.scalar.activation(hf[:, at:at + ROWS], R[:, k, m * ROWS:(m + 1) * ROWS], ACT.Gelu,
                                                 bias=rawA[:, slot, H + HT * D + t:H + HT * D + t + 1])
                    g.then_inc(gelu_bank, 1)
                act.wait_ge(gelu_bank, n * 3 + 2)
                wait(act, f2_bank, (n - 2) * 2 + 2 if not isinstance(n, int) or n >= 2 else 0)
                nc.scalar.activation(hh[:, par, 2:4, :], hidden(par, 1), ACT.Copy).then_inc(h_hi1, 1)

            def slots_hi(jj):
                for q in range(4):
                    x = (xABh, xCh)[q % 2]
                    act.wait_ge(sl_mm, jj * 4 + (q + 1))
                    nc.scalar.activation(images(x, q // 2), slot_bank(q), ACT.Copy).then_inc(sl_hi, 1)

            def x1T(t):
                act.wait_ge(t1_mm, t + 1)
                nc.scalar.activation(xT2[:, 0, P * t:P * t + P], EO[:, 0, 0:P], ACT.Copy)
                nc.scalar.activation(xT2[0:DC, 1, P * t:P * t + P], EO[0:DC, 0, P:2 * P], ACT.Copy).then_inc(x1T_up, 1)

            def qk(t):
                c = slice(P * t, P * t + P)
                if t == 0:
                    act.wait_ge(attn_in, 64)
                    act.wait_ge(phss_mm, 1)
                act.wait_ge(qk_mm, t + 1)
                nc.scalar.activation(qA[:, c], R[:, t, 0:P], ACT.Identity, bias=bqk[:, 0:1])
                nc.scalar.activation(qC[:, c], R[0:DC, t, P:2 * P], ACT.Identity, bias=bqk_c[:, 0:1])
                nc.scalar.activation(kA[:, c], R[:, t, 2 * P:3 * P], ACT.Identity, bias=bqk[:, 1:2])
                nc.scalar.activation(kC[:, c], R[0:DC, t, 3 * P:4 * P], ACT.Identity,
                                     bias=bqk_c[:, 1:2]).then_inc(qk_up, 1)

            def exps(t):
                act.wait_ge(nmx_up, t + 1)
                act.wait_ge(const_up, 4)
                for a in range(2):
                    r = slice(L * a, L * a + L)
                    x = nc.scalar.activation(prob[r, t, L * a:L * a + L], R[r, t, L * a:L * a + L], ACT.Exp,
                                             bias=nmx[r, t:t + 1], accum_out=asum[r, t:t + 1])
                x.then_inc(exp_up, 1)

            def pT(t):
                act.wait_ge(pT_mm, t + 1)
                nc.scalar.activation(probT[:, P * t:P * t + P], R[:, t, P:2 * P], ACT.Copy).then_inc(pT_up, 1)

            def yT(t):
                c = slice(P * t, P * t + P)
                act.wait_ge(y_mm, t + 1)
                nc.scalar.activation(yA[:, c], R[:, t, 2 * P:3 * P], ACT.Copy)
                nc.scalar.activation(yC[:, c], R[0:DC, t, 3 * P:4 * P], ACT.Copy).then_inc(y_up, 1)

            def xnT(t):
                act.wait_ge(t2_mm, t + 1)
                nc.scalar.activation(xT2[:, 0, P * t:P * t + P], EO[:, 1, 0:P], ACT.Copy)
                nc.scalar.activation(xT2[0:DC, 1, P * t:P * t + P], EO[0:DC, 1, P:2 * P], ACT.Copy).then_inc(xnT_up, 1)

            def logits(t):
                act.wait_ge(lgm_up, t + 1)
                nc.scalar.activation(pe_exp[:, t, :], pe_exp[:, t, :], ACT.Exp).then_inc(lge_up, 1)
                act.wait_ge(nM_up, t + 1)
                nc.scalar.activation(tE[:, t, :], mE[:, t, :], ACT.Exp, bias=nM[:, t:t + 1]).then_inc(tE_up, 1)

            def first_weights(t):
                (lambda: w1_split(0, 0, 0, 0), lambda: w2_split(0, 0, 0, 0), lambda: w1_split(1, 1, 1, 0),
                 lambda: None)[t]()

            wave((x1T, 0), (exps, 1), (qk, 0), (pT, 1), (yT, 1), (first_weights, 1), (xnT, 2), (logits, 2))
            nc.scalar.preload_act_table(ACT.Gelu)
            slots_hi(0)
            act.wait_ge(gT_mm, NT)
            nc.scalar.activation(gateT[:, :], EO[0:E, 0, :], ACT.Copy).then_inc(gT_up, 1)
            gelu(0, 0, 0, 0)

            def body(j, first, last):
                for i in range(EG):
                    e = j * EG + i
                    more = not (last and i == EG - 1)
                    if not (last and i >= EG - 2):
                        w1_split(e + 2, i % 2, (i + 2) % EG, j + (i + 2) // EG)
                    if more:
                        gelu(e + 1, (i + 1) % 2, (i + 1) % EG, j + (i + 1) // EG)
                    if more:
                        w2_split(e + 1, (i + 1) % 2, (i + 1) % EG, j + (i + 1) // EG)
                    for r in range(2):
                        act.wait_ge(f2_bank, e * 2 + (r + 1))
                        wait(act, eo_add, e * 2 + (r - 1))
                        nc.scalar.activation(eol[:, r, :], EO[:, r, D:2 * D], ACT.Copy).then_inc(eo_cp, 1)
                        if r == 0:
                            if i == 1:
                                act.wait_ge(cwT_mm, j + 1)
                                wait(act, comb, j)
                                nc.scalar.activation(cwT[:, :], R[:, G, :], ACT.Copy).then_inc(cwT_up, 1)
                            if i == 2 and not last:
                                slots_hi(j + 1)

            groups(act, body)

        @block.vector
        def _(dve):
            links = [0]

            def link(ins):
                links[0] += 1
                ins.then_inc(link_s, 1)
                dve.wait_ge(link_s, links[0])

            def w1_split(e, par, slot, grp):
                dve.wait_ge(w1_hi, e * 2 + 1)
                nc.vector.tensor_tensor(w1l[:, par, :], rawA[:, slot, 0:H], w1h[:, par, :].bitcast(F32), ALU.subtract)
                dve.wait_ge(w1_hi, e * 2 + 2)
                nc.vector.tensor_tensor(w1c[DC:P, par, :], rawC[:, slot, :], w1c[0:DC, par, :].bitcast(F32),
                                        ALU.subtract).then_inc(w1_lo, 1)

            def w2_split(e, par, slot, grp):
                dve.wait_ge(w2_hi, e + 1)
                nc.vector.tensor_tensor(w2s[:, par, :, D:2 * D],
                                        rawA[:, slot, H:H + HT * D].rearrange("p (t d) -> p t d", t=HT),
                                        w2s[:, par, :, 0:D].bitcast(F32), ALU.subtract).then_inc(w2_lo, 1)

            def h_split(n, par):
                wait(dve, f2_bank, (n - 2) * 2 + 2 if not isinstance(n, int) or n >= 2 else 0)

                def hi(k):
                    dve.wait_ge(gelu_bank, n * 3 + (k + 1))
                    nc.vector.tensor_copy(hh[:, par, 2 * k:2 * k + 2, :], hidden(par, k)).then_inc(h_hi, 1)

                def lo(k):
                    nc.vector.tensor_tensor(hl[:, par, 2 * k:2 * k + 2, :], hidden(par, k),
                                            hh[:, par, 2 * k:2 * k + 2, :].bitcast(F32), ALU.subtract).then_inc(h_lo, 1)

                hi(0)
                dve.wait_ge(h_hi, n * 2 + 1)
                lo(0)
                hi(2)
                dve.wait_ge(h_hi1, n + 1)
                lo(1)
                dve.wait_ge(h_hi, n * 2 + 2)
                lo(2)

            def slots_lo(jj):
                for q in range(4):
                    hi, lo = ((xABh, xABl), (xCh, xCl))[q % 2]
                    dve.wait_ge(sl_hi, jj * 4 + (q + 1))
                    nc.vector.tensor_tensor(images(lo, q // 2), slot_bank(q), images(hi, q // 2).bitcast(F32),
                                            ALU.subtract).then_inc(sl_lo, 1)

            def tokens(t):
                dve.wait_ge(tok_mm, t + 1)
                link(nc.vector.tensor_tensor(h[:, t, :], R[:, t, 0:D], rb[:, 0, :], ALU.add))
                link(nc.vector.bn_stats(st[:, t, :], h[:, t, :]))
                link(nc.vector.bn_aggr(mv[:, t, :], st[:, t, :]))
                nc.vector.tensor_scalar(ve[:, t:t + 1], mv[:, t, 1:2], LN_EPS, None, ALU.add).then_inc(ve_up, 1)

            def norm1(t):
                dve.wait_ge(rstd_up, t + 1)
                nc.vector.tensor_scalar(xn[:, t, :], h[:, t, :], mv[:, t, 0:1], rstd[:, t:t + 1], ALU.subtract,
                                        ALU.mult).then_inc(xn1_up, 1)

            def hbias(t):
                dve.wait_ge(xn1_up, t + 1)
                nc.vector.tensor_tensor(h[:, t, :], h[:, t, :], rb[:, 2, :], ALU.add).then_inc(hb_up, 1)

            def vbias(t):
                dve.wait_ge(v_mm, t + 1)
                nc.vector.tensor_tensor(v[:, t, :], EO[:, 0, 2 * P:2 * P + D], rb[:, 1, :], ALU.add).then_inc(v_up, 1)

            def score_max(t):
                dve.wait_ge(sc_mm, t + 1)
                for a in range(2):
                    r = slice(L * a, L * a + L)
                    x = nc.vector.tensor_reduce(nmx[r, t:t + 1], R[r, t, L * a:L * a + L], AX.X, ALU.max, negate=True)
                x.then_inc(nmx_up, 1)

            def probs(t):
                dve.wait_ge(exp_up, t + 1)
                link(nc.vector.reciprocal(arec[:, t:t + 1], asum[:, t:t + 1]))
                nc.vector.tensor_scalar(prob[:, t, :], prob[:, t, :], arec[:, t:t + 1], None,
                                        ALU.mult).then_inc(prob_up, 1)

            def residual(t):
                dve.wait_ge(o_mm, t + 1)
                dve.wait_ge(hb_up, t + 1)
                link(nc.vector.tensor_tensor(h[:, t, :], EO[:, 1, 2 * P:2 * P + D], h[:, t, :], ALU.add))
                link(nc.vector.bn_stats(st[:, t, :], h[:, t, :]))
                link(nc.vector.bn_aggr(mv[:, t, :], st[:, t, :]))
                link(nc.vector.tensor_scalar(pw[:, t, 0:1], mv[:, t, 1:2], LN_EPS, None, ALU.add))
                link(nc.vector.reciprocal(rve[:, t:t + 1], pw[:, t, 0:1]))
                nc.vector.tensor_scalar(pw[:, t, 1:2], mv[:, t, 1:2], rve[:, t:t + 1], L2_EPS2 / D, ALU.mult,
                                        ALU.max).then_inc(pw_up, 1)

            def norm2(t):
                dve.wait_ge(pwr_up, t + 1)
                link(nc.vector.tensor_scalar(f2n[:, t:t + 1], pwr[:, t, 0:1], pwr[:, t, 1:2], float(D) ** -0.5,
                                             ALU.mult, ALU.mult))
                nc.vector.tensor_scalar(xn[:, t, :], h[:, t, :], mv[:, t, 0:1], f2n[:, t:t + 1], ALU.subtract,
                                        ALU.mult).then_inc(xn2_up, 1)

            def bc(x):
                return x.unsqueeze(2).broadcast_to([P, E, S])

            def less_max(t):
                lg = logit_banks(t).rearrange("p a (e s) -> p (a e) s", s=S)
                dve.wait_ge(lg_mm, t + 1)
                link(nc.vector.tensor_reduce(mE[:, t, :], lg, AX.X, ALU.max))
                nc.vector.tensor_tensor(pe_exp[:, t, :].rearrange("p (e s) -> p e s", s=S), lg, bc(mE[:, t, :]),
                                        ALU.subtract).then_inc(lgm_up, 1)
                nc.vector.tensor_reduce(nM[:, t:t + 1], mE[:, t, :], AX.X, ALU.max, negate=True).then_inc(nM_up, 1)

            def sums(t):
                dve.wait_ge(lge_up, t + 1)
                link(nc.vector.tensor_reduce(sE[:, t, :], pe_exp[:, t, :].rearrange("p (e s) -> p e s", s=S), AX.X,
                                             ALU.add))
                nc.vector.reciprocal(rE[:, t, :], sE[:, t, :]).then_inc(rE_up, 1)

            def phi_diagonals():
                dve.wait_ge(pinv_up, 1)
                dve.wait_ge(id_up, 2)
                for c in range(E * S // P):
                    nc.vector.tensor_scalar(dsc[:, c, :], ident[:, :], pinv[:, c:c + 1], scl[:, 0:1], ALU.mult,
                                            ALU.mult).then_inc(dsc_up, 1)

            def phi_scale():
                dve.wait_ge(dsc_mm, E * S // P)
                flat = Y[:, :, :].rearrange("p a n -> p (a n)")
                nc.vector.tensor_tensor(phA[:, :], flat, phA[:, :], ALU.mult)
                nc.vector.tensor_tensor(phC[:, :], flat[0:DC, :], phC[:, :], ALU.mult).then_inc(phin_up, 1)

            def first_weights(t):
                (lambda: None, lambda: w1_split(0, 0, 0, 0), lambda: w2_split(0, 0, 0, 0),
                 lambda: w1_split(1, 1, 1, 0))[t]()

            dve.wait_ge(phss_mm, 1)
            nc.vector.tensor_scalar(pss[:, :], Y[:, 0, 0:E * S // P], L2_EPS2, None, ALU.max).then_inc(phss_up, 1)
            dve.wait_ge(bias_in, 32)
            tokens(0)
            tokens(1)
            norm1(0)
            wave((lambda t: phi_diagonals() if t == 0 else None, 0),
                 (score_max, 1), (probs, 1),
                 (lambda t: tokens(t + 2) if t + 2 < NT else None, 0),
                 (lambda t: norm1(t + 1) if t + 1 < NT else None, 0),
                 (hbias, 0),
                 (vbias, 0),
                 (lambda t: phi_scale() if t == 0 else None, 0),
                 (residual, 1), (first_weights, 1), (norm2, 1), (less_max, 2), (sums, 2))
            dve.wait_ge(tE_up, NT)
            dve.wait_ge(rE_up, NT)
            link(nc.vector.tensor_tensor(uE[:, :, :], sE[:, :, :], tE[:, :, :], ALU.mult))
            link(nc.vector.tensor_reduce(uS[:, :], uE[:, :, :], AX.X, ALU.add))
            link(nc.vector.reciprocal(ru[:, :], uS[:, :]))
            rub = ru[:, :].unsqueeze(2).broadcast_to([P, NT, E])
            nc.vector.tensor_tensor(gate[:, :, :], uE[:, :, :], rub, ALU.mult)
            nc.vector.tensor_tensor(gexp[:, :, :], tE[:, :, :], rub, ALU.mult).then_inc(gate_up, 1)
            slots_lo(0)
            h_split(0, 0)

            def body(j, first, last):
                for i in range(EG):
                    e = j * EG + i
                    more = not (last and i == EG - 1)
                    if not (last and i >= EG - 2):
                        w1_split(e + 2, i % 2, (i + 2) % EG, j + (i + 2) // EG)
                    if more:
                        h_split(e + 1, (i + 1) % 2)
                    if more and i != 2:
                        w2_split(e + 1, (i + 1) % 2, (i + 1) % EG, j + (i + 1) // EG)
                    for r in range(2):
                        dve.wait_ge(eo_cp, e * 2 + (r + 1))
                        if not (first and i == 0):
                            dve.wait_ge(eo_in[(i - 1) % EG], (j + 1 if i else j) * EO_IN)
                        nc.vector.tensor_tensor(eot[:, r, :], EO[:, r, 0:D], eol[:, r, :], ALU.add).then_inc(eo_add, 1)
                        if r == 0 and i == 2:
                            if not last:
                                slots_lo(j + 1)
                            w2_split(e + 1, (i + 1) % 2, (i + 1) % EG, j + (i + 1) // EG)

            groups(dve, body)
            dve.wait_ge(comb, NG)
            for t in range(2):
                nc.vector.tensor_tensor(xn[:, 2 * t:2 * t + 2, :],
                                        Y[:, t, 0:2 * D].rearrange("p (a d) -> p a d", a=2),
                                        h[:, 2 * t:2 * t + 2, :], ALU.add).then_inc(fin_up, 1)

        @block.tensor
        def _(pe):
            mm = nc.tensor.matmul

            pe.wait_ge(phsq_up, 1)
            pe.wait_ge(const_up, 4)
            for c in range(E * S // P):
                mm(Y[:, 0, c:c + 1], phsq[:, P * c:P * c + P], ones[:, 0:1], start=True, stop=False)
                x = mm(Y[:, 0, c:c + 1], phsqC[:, P * c:P * c + P], ones[0:DC, 0:1], start=False, stop=True)
            x.then_inc(phss_mm, 1)

            def tok(t):
                for k in range(PK):
                    x = mm(R[:, t, 0:D], xTs[:, k, P * t:P * t + P], wtk[:, k, :], start=(k == 0), stop=(k == PK - 1))
                x.then_inc(tok_mm, 1)

            def transposes(bank, src, t, done):
                nc.tensor.transpose(bank[:, 0:P], src[:, t, 0:P], ident[:, :])
                nc.tensor.transpose(bank[0:DC, P:2 * P], src[:, t, P:D], ident[:, :]).then_inc(done, 1)

            def norm_rows(t):
                if t == 0:
                    pe.wait_ge(phss_up, 1)
                    for c8 in range(E * S // P):
                        pe.wait_ge(dsc_up, c8 + 1)
                        mm(Y[:, c8 // 4, P * (c8 % 4):P * (c8 % 4) + P], ones[:, :], dsc[:, c8, :],
                           start=True, stop=True).then_inc(dsc_mm, 1)

            def t1(t):
                pe.wait_ge(xn1_up, t + 1)
                wait(pe, v_up, t)
                transposes(EO[:, 0, :], xn, t, t1_mm)

            def qk(t):
                c = slice(P * t, P * t + P)
                pe.wait_ge(x1T_up, t + 1)
                pe.wait_ge(attn_in, 64)
                for w in range(2):
                    at = 2 * P * w
                    mm(R[:, t, at:at + P], wat[:, w, 0:P], xT2[:, 0, c], start=True, stop=False)
                    mm(R[:, t, at:at + P], watC[:, w, 0:P], xT2[0:DC, 1, c], start=False, stop=True)
                    mm(R[0:DC, t, at + P:at + 2 * P], wat[:, w, P:D], xT2[:, 0, c], start=True, stop=False)
                    x = mm(R[0:DC, t, at + P:at + 2 * P], watC[:, w, P:D], xT2[0:DC, 1, c], start=False, stop=True)
                x.then_inc(qk_mm, 1)

            def vv(t):
                c = slice(P * t, P * t + P)
                mm(EO[:, 0, 2 * P:2 * P + D], xT2[:, 0, c], wat[:, 2, :], start=True, stop=False)
                mm(EO[:, 0, 2 * P:2 * P + D], xT2[0:DC, 1, c], watC[:, 2, :], start=False, stop=True).then_inc(v_mm, 1)

            def scores(t):
                c = slice(P * t, P * t + P)
                pe.wait_ge(qk_up, t + 1)
                mm(R[:, t, 0:P], qA[:, c], kA[:, c], start=True, stop=False)
                mm(R[:, t, 0:P], qC[:, c], kC[:, c], start=False, stop=True).then_inc(sc_mm, 1)

            def pT(t):
                pe.wait_ge(prob_up, t + 1)
                nc.tensor.transpose(R[:, t, P:2 * P], prob[:, t, :], ident[:, :]).then_inc(pT_mm, 1)

            def yT(t):
                c = slice(P * t, P * t + P)
                pe.wait_ge(pT_up, t + 1)
                pe.wait_ge(v_up, t + 1)
                mm(R[:, t, 2 * P:3 * P], v[:, t, 0:P], probT[:, c], start=True, stop=True)
                mm(R[0:DC, t, 3 * P:4 * P], v[:, t, P:D], probT[:, c], start=True, stop=True).then_inc(y_mm, 1)

            def proj(t):
                c = slice(P * t, P * t + P)
                pe.wait_ge(y_up, t + 1)
                wait(pe, xnT_up, t)
                mm(EO[:, 1, 2 * P:2 * P + D], yA[:, c], wat[:, 3, :], start=True, stop=False)
                mm(EO[:, 1, 2 * P:2 * P + D], yC[:, c], watC[:, 3, :], start=False, stop=True).then_inc(o_mm, 1)

            def t2(t):
                pe.wait_ge(xn2_up, t + 1)
                transposes(EO[:, 1, :], xn, t, t2_mm)

            def logits(t):
                c = slice(P * t, P * t + P)
                pe.wait_ge(phin_up, 1)
                pe.wait_ge(xnT_up, t + 1)
                wait(pe, lgm_up, t - 1)
                for a in range(2):
                    bank = logit_banks(t)[:, a, :]
                    mm(bank, xT2[:, 0, c], phA[:, 512 * a:512 * a + 512], start=True, stop=False)
                    x = mm(bank, xT2[0:DC, 1, c], phC[:, 512 * a:512 * a + 512], start=False, stop=True)
                x.then_inc(lg_mm, 1)

            pe.wait_ge(tok_in, 48)
            tok(0)
            tok(1)
            wave((t1, 0), (scores, 1), (lambda t: tok(t + 2) if t + 2 < NT else None, 0), (norm_rows, 0),
                 (qk, 0), (pT, 1), (vv, 0), (t2, 2), (yT, 1), (logits, 2), (proj, 1))

            def slots(jj):
                pe.wait_ge(dwn_up, jj * NT + NT)
                for q in range(4):
                    part = (slice(0, P), slice(P, 2 * P))[q % 2]
                    if q == 0:
                        wait(pe, cwT_up, jj)
                    else:
                        wait(pe, gelu_bank, jj * 12 + (q - 3))
                    for b in range(4):
                        bi = 4 * (q // 2) + b
                        x = mm(R[:, (G, 0, 1, 2)[q], GC * b:GC * b + GC], xnp[:, bi, part],
                               dwn[:, bi // 2, :], start=True, stop=True)
                    x.then_inc(sl_mm, 1)

            def f1(n, par, slot):
                pe.wait_ge(w1_lo, n + 1)
                for k in range(3):
                    wait(pe, gelu_bank, (n - 1) * 3 + (k + 1) if not isinstance(n, int) or n >= 1 else 0)
                    for m in range(2):
                        t = 2 * k + m
                        c = slice(P * t, P * t + P)
                        o = R[:, k, m * ROWS:(m + 1) * ROWS]
                        mm(o, w1h[:, par, c], xABh[:, slot, :], start=True, stop=False)
                        mm(o, w1h[:, par, c], xABl[:, slot, :], start=False, stop=False)
                        mm(o, w1l[:, par, c], xABh[:, slot, :], start=False, stop=False)
                        mm(o, w1c[:, par, c], xCh[:, slot, :], start=False, stop=False)
                        x = mm(o, w1c[:, par, c], xCl[:, slot, :], start=False, stop=True)
                    x.then_inc(f1_bank, 1)

            def f2(e, par, r):
                if r == 0:
                    pe.wait_ge(h_lo, e * 3 + 3)
                    pe.wait_ge(w2_lo, e + 1)
                wait(pe, eo_add, e * 2 + (r - 1))
                for t in range(HT):
                    rows = slice(P * r, P * r + P)
                    mm(EO[:, r, 0:2 * D], hh[:, par, t, rows], w2s[:, par, t, :], start=(t == 0), stop=False)
                    x = mm(EO[:, r, 0:D], hl[:, par, t, rows], w2s[:, par, t, 0:D], start=False, stop=(t == HT - 1))
                x.then_inc(f2_bank, 1)

            def combine(j, last):
                for i in range(EG):
                    pe.wait_ge(eo_in[i], j * EO_IN + EO_IN)
                pe.wait_ge(cwT_up, j + 1)
                for b in range(B):
                    half, at = L * (b % 2), D * ((b // 2) % 2)
                    x = mm(Y[half:half + L, b // 4, at:at + D], cwT[:, L * b:L * b + L], eog[:, b, :],
                           start=False, stop=last, skip_group_check=True)
                x.then_inc(comb, 1)

            pe.wait_ge(xnp_up, B)
            pe.wait_ge(lgm_up, NT)
            slots(0)
            pe.wait_ge(gate_up, 1)
            for t in range(NT):
                nc.tensor.transpose(EO[0:E, 0, P * t:P * t + P], gate[:, t, :], ident[:, :]).then_inc(gT_mm, 1)
            pe.wait_ge(sl_lo, 4)
            f1(0, 0, 0)
            pe.wait_ge(gT_up, 1)
            pe.wait_ge(b2_in, 16)
            for t in range(NT):
                mm(Y[:, t // 2, D * (t % 2):D * (t % 2) + D], gateT[:, P * t:P * t + P], b2s[:, :],
                   start=(t % 2 == 0), stop=False, skip_group_check=True)

            def body(j, first, last):
                for i in range(EG):
                    e = j * EG + i
                    if not (last and i == EG - 1):
                        if i == EG - 1:
                            pe.wait_ge(sl_lo, j * 4 + 8)
                        f1(e + 1, (i + 1) % 2, (i + 1) % EG)
                    f2(e, i % 2, 0)
                    if i == 0 and not first:
                        combine(j - 1, False)
                    if i == 1:
                        pe.wait_ge(cws_up, j + 1)
                        pe.wait_ge(sl_lo, j * 4 + 4)
                        for t in range(NT):
                            x = nc.tensor.transpose(R[:, G, P * t:P * t + P], cws[:, t, :], ident[:, :])
                        x.then_inc(cwT_mm, 1)
                    if i == 2 and not last:
                        slots(j + 1)
                    f2(e, i % 2, 1)

            groups(pe, body)
            combine(NG - 1, True)


_INS = ["xT", "wtokT", "rowbias", "wattnAB", "wattnC", "bqkAB", "bqkC", "phi", "scale", "b2", "wA", "wC"]


def kernel(**inputs):
    import numpy as np
    import concourse.bacc as bacc
    from concourse.bass_utils import run_bass_kernel_spmd

    def t(name):
        return np.asarray(inputs[name])

    x = t("x").reshape(B, 3, L, 2, P).transpose(4, 1, 3, 0, 2).reshape(P, PK, B * L)
    wtok = t("L0_tok_W").T.reshape(PK, P, D).transpose(1, 0, 2)
    attn = np.stack([t(f"L0_attn_w{c}").T for c in "qkvo"], axis=1)
    bqk = np.stack([t("L0_attn_bq"), t("L0_attn_bk")], axis=1)
    w1, b1, w2 = t("L0_ffn_w1"), t("L0_ffn_b1"), t("L0_ffn_w2")
    w2p = w2.reshape(E, HT, P, D).transpose(0, 2, 1, 3).reshape(E, P, HT * D)
    b1p = b1.reshape(E, HT, P).transpose(0, 2, 1)
    arrays = {
        "xT": x,
        "wtokT": wtok,
        "rowbias": np.stack([t("L0_tok_b"), t("L0_attn_bv"), t("L0_attn_bo")]),
        "wattnAB": attn[:P],
        "wattnC": attn[P:],
        "bqkAB": bqk[:P],
        "bqkC": bqk[P:],
        "phi": t("L0_ffn_phi").reshape(D, E * S),
        "scale": t("L0_ffn_scale"),
        "b2": t("L0_ffn_b2"),
        "wA": np.concatenate([w1[:, :P, :], w2p, b1p], axis=2),
        "wC": w1[:, P:, :],
    }
    arrays = {k: np.ascontiguousarray(a) for k, a in arrays.items()}
    nc = bacc.Bacc("TRN2", target_bir_lowering=False, num_devices=1)
    args = [nc.dram_tensor(f"{k}_dram", arrays[k].shape, mybir.dt.from_np(arrays[k].dtype), kind="ExternalInput").ap()
            for k in _INS]
    args.append(nc.dram_tensor("out_dram", (B, L, D), F32, kind="ExternalOutput").ap())
    vit_block(nc, *args)
    r = run_bass_kernel_spmd(nc, [{f"{k}_dram": arrays[k] for k in _INS}], core_ids=[0])
    return r.results[0]["out_dram"]
```

```python
import concourse.bass as bass
from concourse import mybir
from contextlib import ExitStack

F32 = mybir.dt.float32
F32R = mybir.dt.float32r
ALU = mybir.AluOpType
ACT = mybir.ActivationFunctionType
AX = mybir.AxisListType

P = 128
B, L, D = 8, 64, 192
DC = D - P
NT = B * L // P
PK = 6
E, S, H = 32, 32, 768
HT = H // P
ROWS = S * B
EG = 4
NG = E // EG
GC = EG * S
EO_IN = 2 * 16
LN_EPS = 1e-5
L2_EPS2 = 1e-24
WARM_UP = 10
SB = S // 2


def vit_block(nc, xT, wtokT, rowbias, wattnAB, wattnC, bqkAB, bqkC, phi, scale, b2, wA, wC, out):
    out_v = out.rearrange("b l d -> (b l) d").rearrange("(t p) d -> p t d", p=P)

    ctx = ExitStack()
    with ctx:
        def sb(name, shape, dt=F32):
            return ctx.enter_context(nc.sbuf_tensor(name, shape, dt))

        def sem(name):
            return ctx.enter_context(nc.semaphore(name))

        rawA = sb("rawA", [P, EG, H + HT * D + HT])
        rawC = sb("rawC", [DC, EG, H])
        w1h = sb("w1h", [P, 2, H], F32R)
        w1l = sb("w1l", [P, 2, H], F32R)
        w1c = sb("w1c", [P, 2, H], F32R)
        w2s = sb("w2s", [P, 2, HT, 2 * D], F32R)
        xABh = sb("xABh", [P, EG, ROWS], F32R)
        xABl = sb("xABl", [P, EG, ROWS], F32R)
        xCh = sb("xCh", [P, EG, ROWS], F32R)
        xCl = sb("xCl", [P, EG, ROWS], F32R)
        hf = sb("hf", [P, 2 * HT * ROWS])
        hh = sb("hh", [P, 2, HT, ROWS], F32R)
        hl = sb("hl", [P, 2, HT, ROWS], F32R)
        eol = sb("eol", [P, 2, D])
        eot = sb("eot", [P, 2, D])
        eog = sb("eog", [P, B, D])
        cws = sb("cws", [P, NT, GC])
        cwT = sb("cwT", [P, NT * P])
        dwn = sb("dwn", [P, NT, GC])
        pe_exp = sb("pe_exp", [P, NT, E * S])
        gate = sb("gate", [P, NT, E])
        gexp = sb("gexp", [P, NT, E])
        gateT = sb("gateT", [E, NT * P])
        xnp = sb("xnp", [P, B, D + DC])
        ident = sb("ident", [P, P])
        ones = sb("ones", [P, P])
        mhalf = sb("mhalf", [P, E * S // P])
        h = sb("h", [P, NT, D])
        xn = sb("xn", [P, NT, D])
        xT2 = sb("xT2", [P, 2, NT * P])
        v = sb("v", [P, NT, D])
        rb = sb("rb", [P, 3, D])
        wat = sb("wat", [P, 4 * D])
        watC = sb("watC", [DC, 4 * D])
        bqk = sb("bqk", [P, 2])
        bqk_c = sb("bqk_c", [DC, 2])
        phA = sb("phA", [P, E * S])
        phC = sb("phC", [DC, E * S])
        scl = sb("scl", [P, 1])
        b2s = sb("b2s", [E, D])
        st = sb("st", [P, NT, 6])
        mv = sb("mv", [P, NT, 2])
        ve = sb("ve", [P, NT])
        rstd = sb("rstd", [P, NT])
        pw = sb("pw", [P, NT])
        pwr = sb("pwr", [P, NT])
        pss = sb("pss", [P, E * S // P])
        pinv = sb("pinv", [P, E * S // P])
        nmx = sb("nmx", [P, NT])
        asum = sb("asum", [P, NT])
        arec = sb("arec", [P, NT])
        mE = sb("mE", [P, NT, E])
        nM = sb("nM", [P, NT])
        tE = sb("tE", [P, NT, E])
        sE = sb("sE", [P, NT, E])
        rE = sb("rE", [P, NT, E])
        uE = sb("uE", [P, NT, E])
        uS = sb("uS", [P, NT])
        ru = sb("ru", [P, NT])

        xTs = pe_exp[:, 0:3, :].rearrange("p a n -> p (a n)").rearrange("p (k t) -> p k t", k=PK)
        phsq = pe_exp[:, 3, :]
        wtk = eog[:, 0:PK, :]
        qA, kA = hf[:, 0:512], hf[:, 512:1024]
        qC, kC = hf[0:DC, 1024:1536], hf[0:DC, 1536:2048]
        yA, yC = hf[:, 2048:2560], hf[0:DC, 2560:3072]
        phsqC = hf[0:DC, 2048:3072]
        dsc = phsq.rearrange("p (c n) -> p c n", n=P)
        phAh, phAl = (hh[:, a, 0:4, :].rearrange("p t r -> p (t r)") for a in range(2))
        phCs = hl[:, 0, 0:4, :].rearrange("p t r -> p (t r)")
        uABh, uABl, uCh, uCl = (x[:, 0:2, :].rearrange("p a r -> p (a r)") for x in (xABh, xABl, xCh, xCl))
        prob = cws
        probT = cwT

        R = ctx.enter_context(nc.psum_tensor("R", [P, 4, 512], F32))
        EO = ctx.enter_context(nc.psum_tensor("EO", [P, 2, 512], F32))
        Y = ctx.enter_context(nc.psum_tensor("Y", [P, 2, 512], F32))
        G = 3

        wtok_in, bias_in, attn_in, phi_in, b2_in = (sem(n) for n in ("wtok_in", "bias_in", "attn_in", "phi_in", "b2_in"))
        tok_in = [sem(f"tok_in{t}") for t in range(NT)]
        w1_in = [sem(f"w1_in{s}") for s in range(EG)]
        w2_in = [sem(f"w2_in{s}") for s in range(EG)]
        eo_in = [sem(f"eo_in{s}") for s in range(EG)]
        out_done = sem("out_done")
        const_up, id_up = sem("const_up"), sem("id_up")
        tok_mm, ve_up, rstd_up, xn1_up = (sem(n) for n in ("tok_mm", "ve_up", "rstd_up", "xn1_up"))
        t1_mm, x1T_up, qk_mm, v_mm, qk_up, v_up = (sem(n) for n in ("t1_mm", "x1T_up", "qk_mm", "v_mm", "qk_up", "v_up"))
        sc_mm, nmx_up, exp_up, prob_up, pT_mm, pT_up = (sem(n) for n in ("sc_mm", "nmx_up", "exp_up", "prob_up", "pT_mm", "pT_up"))
        y_mm, y_up, o_mm, pw_up, pwr_up = (sem(n) for n in ("y_mm", "y_up", "o_mm", "pw_up", "pwr_up"))
        xn2_up, t2_mm, xnT_up, xnp_up, fin_up = (sem(n) for n in ("xn2_up", "t2_mm", "xnT_up", "xnp_up", "fin_up"))
        phsq_up, phss_mm, phss_up, pinv_up, dsc_up, dsc_mm, phin_up = (
            sem(n) for n in ("phsq_up", "phss_mm", "phss_up", "pinv_up", "dsc_up", "dsc_mm", "phin_up"))
        phsum_up, phh_up, phlA_up, phlC_up, xnh_up = (sem(n) for n in ("phsum_up", "phh_up", "phlA_up", "phlC_up", "xnh_up"))
        lg_mm, lgm_up, lge_up, nM_up, tE_up, rE_up, gate_up, gT_mm, gT_up = (
            sem(n) for n in ("lg_mm", "lgm_up", "lge_up", "nM_up", "tE_up", "rE_up", "gate_up", "gT_mm", "gT_up"))
        link_s = sem("dve_link")
        w1_hi, w1_lo, w2_hi, w2_lo = (sem(n) for n in ("w1_hi", "w1_lo", "w2_hi", "w2_lo"))
        f1_bank, gelu_bank, h_hi, h_hi1, h_lo = (sem(n) for n in ("f1_bank", "gelu_bank", "h_hi", "h_hi1", "h_lo"))
        f2_bank, eo_cp, eo_add = (sem(n) for n in ("f2_bank", "eo_cp", "eo_add"))
        cws_up, cwT_mm, cwT_up, comb = (sem(n) for n in ("cws_up", "cwT_mm", "cwT_up", "comb"))
        dwn_up, half_comb = sem("dwn_up"), sem("half_comb")
        sl_mm, sl_hi, sl_lo = (sem(n) for n in ("sl_mm", "sl_hi", "sl_lo"))

        block = ctx.enter_context(nc.Block())

        def wait(eng, s, value):
            if not isinstance(value, int) or value > 0:
                eng.wait_ge(s, value)

        def groups(eng, body):
            body(0, True, False)
            with eng.Fori(1, NG - 1) as j:
                body(j, False, False)
            body(NG - 1, False, True)

        def load(slot, e):
            nc.sync.dma_start(rawA[:, slot, 0:H], wA[bass.ds(e, 1), :, 0:H]).then_inc(w1_in[slot], 16)
            nc.sync.dma_start(rawC[:, slot, :], wC[bass.ds(e, 1), :, :]).then_inc(w1_in[slot], 16)
            nc.sync.dma_start(rawA[:, slot, H:], wA[bass.ds(e, 1), :, H:]).then_inc(w2_in[slot], 16)

        def hidden(par, k):
            at = (par * HT + 2 * k) * ROWS
            return hf[:, at:at + 2 * ROWS].rearrange("p (t r) -> p t r", t=2)

        def slot_bank(q):
            return R[:, (G, 0, 1, 2)[q], :].rearrange("p (b n) -> p n b", b=4)

        def images(x, half):
            return x[:, :, :].rearrange("p e (s b) -> p (e s) b", b=B)[:, :, 4 * half:4 * half + 4]

        def logit_banks(t):
            return EO[:, :, :] if t == 2 else Y[:, :, :]

        def turns(*stages):
            order = [(place, stage, t) for stage, places in stages for t, place in enumerate(places)]
            for _, stage, t in sorted(order, key=lambda turn: turn[0]):
                stage(t)

        @block.sync
        def _(sp):
            def tokens_in(t):
                c = slice(P * t, P * t + P)
                sp.dma_start(xTs[:, :, c], xT[:, :, c]).then_inc(tok_in[t], 16)

            sp.dma_start(wtk, wtokT).then_inc(wtok_in, 16)
            tokens_in(0)
            sp.dma_start(rb[:, :, :], rowbias.partition_broadcast(P)).then_inc(bias_in, 16)
            sp.dma_start(scl[:, :], scale.partition_broadcast(P)).then_inc(bias_in, 16)
            sp.dma_start(phA[:, :], phi[0:P, :]).then_inc(phi_in, 16)
            sp.dma_start(phC[:, :], phi[P:D, :]).then_inc(phi_in, 16)
            sp.dma_start(wat[:, :], wattnAB).then_inc(attn_in, 16)
            sp.dma_start(watC[:, :], wattnC).then_inc(attn_in, 16)
            sp.dma_start(bqk[:, :], bqkAB).then_inc(attn_in, 16)
            sp.dma_start(bqk_c[:, :], bqkC).then_inc(attn_in, 16)
            for t in range(1, NT):
                tokens_in(t)
            for e in range(EG):
                load(e, e)
            sp.dma_start(b2s[:, :], b2).then_inc(b2_in, 16)

            def body(j, first, last):
                for i in range(EG):
                    e = j * EG + i
                    for r in range(2):
                        sp.wait_ge(eo_add, e * 2 + (r + 1))
                        if i == 0 and r == 0:
                            wait(sp, comb, j)
                        at = S * i + SB * r
                        sp.dma_start(eog[at:at + SB, :, :], eot[:, r, :]).then_inc(eo_in[i], 16)
                    if not last:
                        sp.wait_ge(w1_lo, e + 1)
                        sp.wait_ge(w2_lo, e + 1)
                        sp.wait_ge(gelu_bank, e * 3 + 3)
                        load(i, e + EG)

            groups(sp, body)
            for t in range(2):
                sp.wait_ge(fin_up, t + 1)
                sp.dma_start(out_v[:, 2 * t:2 * t + 2, :], xn[:, 2 * t:2 * t + 2, :]).then_inc(out_done, 16)
            sp.wait_ge(out_done, 32)

        @block.gpsimd
        def _(pool):
            nc.gpsimd.memset(ident[:, :], 0.0).then_inc(id_up, 1)
            nc.gpsimd.memset(ones[:, :], 1.0).then_inc(const_up, 1)
            nc.gpsimd.memset(mhalf[:, :], -0.5).then_inc(const_up, 1)
            pool.wait_ge(id_up, 1)
            nc.gpsimd.affine_select(out=ident[:, :], in_=ident[:, :], compare_op=ALU.not_equal, fill=1.0, base=0,
                                    pattern=[[-1, P]], channel_multiplier=1).then_inc(id_up, 1)
            nc.gpsimd.memset(prob[:, :, :], 0.0).then_inc(const_up, 1)
            nc.gpsimd.memset(xnp[:, :, :], 0.0).then_inc(const_up, 1)
            pool.wait_ge(const_up, 4)

            def phi_pow(_):
                pool.wait_ge(phss_up, 1)
                nc.gpsimd.tensor_tensor(pinv[:, :], pss[:, :], mhalf[:, :], ALU.pow).then_inc(pinv_up, 1)

            def pow1(t):
                pool.wait_ge(ve_up, t + 1)
                nc.gpsimd.tensor_tensor(rstd[:, t:t + 1], ve[:, t:t + 1], mhalf[:, 0:1], ALU.pow).then_inc(rstd_up, 1)

            def pow2(t):
                pool.wait_ge(pw_up, t + 1)
                nc.gpsimd.tensor_tensor(pwr[:, t:t + 1], pw[:, t:t + 1], mhalf[:, 0:1], ALU.pow).then_inc(pwr_up, 1)

            def phi_lo(_):
                pool.wait_ge(phh_up, 1)
                nc.gpsimd.tensor_tensor(phAl, phA[:, :], phAh.bitcast(F32), ALU.subtract).then_inc(phlA_up, 1)

            def experts_of(x, j, t):
                return x[:, t, bass.ds(j * EG, EG)].unsqueeze(2).broadcast_to([P, EG, S])

            def weights(dst, j, t, scales):
                return nc.gpsimd.tensor_tensor(
                    dst[:, t, :].rearrange("p (e s) -> p e s", s=S),
                    pe_exp[:, t, bass.ds(j * GC, GC)].rearrange("p (e s) -> p e s", s=S),
                    experts_of(scales, j, t), ALU.mult)

            def first_dwn(t):
                pool.wait_ge(rE_up, t + 1)
                weights(dwn, 0, t, rE).then_inc(dwn_up, 1)

            turns((pow1, (3, 13, 22, 35)), (phi_pow, (31,)), (pow2, (74, 91, 96, 113)), (phi_lo, (76,)),
                  (first_dwn, (116, 130, 136, 139)))
            pool.wait_ge(gate_up, 1)

            def body(j, first, last):
                for i in range(2):
                    if i == 0:
                        wait(pool, cwT_mm, j)
                        for t in range(NT):
                            x = weights(cws, j, t, gexp)
                        x.then_inc(cws_up, 1)
                    if i == 1 and not last:
                        pool.wait_ge(sl_mm, j * 4 + 4)
                        for t in range(NT):
                            weights(dwn, j + 1, t, rE).then_inc(dwn_up, 1)

            groups(pool, body)

        @block.scalar
        def _(act):
            def phi_squares(_):
                act.wait_ge(phi_in, 32)
                nc.scalar.activation(phsqC, phC[:, :], ACT.Square)
                nc.scalar.activation(phsq, phA[:, :], ACT.Square).then_inc(phsq_up, 1)

            def spread(t):
                if t == 0:
                    act.wait_ge(const_up, 4)
                act.wait_ge(xn2_up, t + 1)
                for a in range(2):
                    r = slice(L * a, L * a + L)
                    nc.scalar.activation(xnp[r, 2 * t + a, 0:D], xn[r, t, :], ACT.Copy)
                    nc.scalar.activation(xnp[r, 2 * t + a, D:], xn[r, t, P:D], ACT.Copy).then_inc(xnp_up, 1)

            def w1_split(e, par, slot, grp):
                act.wait_ge(w1_in[slot], grp * 32 + 32)
                wait(act, f1_bank, (e - 2) * 3 + 3 if not isinstance(e, int) or e >= 2 else 0)
                nc.scalar.activation(w1h[:, par, :], rawA[:, slot, 0:H], ACT.Copy).then_inc(w1_hi, 1)
                nc.scalar.activation(w1c[0:DC, par, :], rawC[:, slot, :], ACT.Copy).then_inc(w1_hi, 1)

            def w2_split(e, par, slot, grp):
                act.wait_ge(w2_in[slot], grp * 16 + 16)
                wait(act, f2_bank, (e - 2) * 2 + 2 if not isinstance(e, int) or e >= 2 else 0)
                nc.scalar.activation(w2s[:, par, :, 0:D],
                                     rawA[:, slot, H:H + HT * D].rearrange("p (t d) -> p t d", t=HT),
                                     ACT.Copy).then_inc(w2_hi, 1)

            def gelu(n, par, slot, grp):
                act.wait_ge(w2_in[slot], grp * 16 + 16)
                wait(act, h_lo, (n - 2) * 3 + 3 if not isinstance(n, int) or n >= 2 else 0)
                for k in range(3):
                    act.wait_ge(f1_bank, n * 3 + (k + 1))
                    for m in range(2):
                        t = 2 * k + m
                        at = par * HT * ROWS + t * ROWS
                        g = nc.scalar.activation(hf[:, at:at + ROWS], R[:, k, m * ROWS:(m + 1) * ROWS], ACT.Gelu,
                                                 bias=rawA[:, slot, H + HT * D + t:H + HT * D + t + 1])
                    g.then_inc(gelu_bank, 1)
                act.wait_ge(gelu_bank, n * 3 + 2)
                wait(act, f2_bank, (n - 2) * 2 + 2 if not isinstance(n, int) or n >= 2 else 0)
                nc.scalar.activation(hh[:, par, 2:4, :], hidden(par, 1), ACT.Copy).then_inc(h_hi1, 1)

            def slots_hi(jj, half=None):
                for q in range(4) if half is None else (2 * half, 2 * half + 1):
                    x = (xABh, xCh)[q % 2]
                    act.wait_ge(sl_mm, jj * 4 + (q + 1))
                    nc.scalar.activation(images(x, q // 2), slot_bank(q), ACT.Copy).then_inc(sl_hi, 1)

            def values(t):
                act.wait_ge(v_mm, t + 1)
                nc.scalar.activation(v[:, t, :], EO[:, t % 2, 2 * P:2 * P + D], ACT.Copy).then_inc(v_up, 1)

            def x1T(t):
                act.wait_ge(t1_mm, t + 1)
                nc.scalar.activation(xT2[:, 0, P * t:P * t + P], EO[:, t % 2, 0:P], ACT.Copy)
                nc.scalar.activation(xT2[0:DC, 1, P * t:P * t + P], EO[0:DC, t % 2, P:2 * P],
                                     ACT.Copy).then_inc(x1T_up, 1)

            def qk(t):
                c = slice(P * t, P * t + P)
                if t == 0:
                    act.wait_ge(attn_in, 64)
                act.wait_ge(qk_mm, t + 1)
                nc.scalar.activation(qA[:, c], R[:, t, 0:P], ACT.Identity, bias=bqk[:, 0:1])
                nc.scalar.activation(qC[:, c], R[0:DC, t, 2 * P:3 * P], ACT.Identity, bias=bqk_c[:, 0:1])
                nc.scalar.activation(kA[:, c], R[:, t, P:2 * P], ACT.Identity, bias=bqk[:, 1:2])
                nc.scalar.activation(kC[:, c], R[DC:P, t, 2 * P:3 * P], ACT.Identity,
                                     bias=bqk_c[:, 1:2]).then_inc(qk_up, 1)

            def exps(t):
                act.wait_ge(nmx_up, t + 1)
                act.wait_ge(const_up, 4)
                for a in range(2):
                    r = slice(L * a, L * a + L)
                    x = nc.scalar.activation(prob[r, t, L * a:L * a + L], R[r, t, L * a:L * a + L], ACT.Exp,
                                             bias=nmx[r, t:t + 1], accum_out=asum[r, t:t + 1])
                x.then_inc(exp_up, 1)

            def pT(t):
                act.wait_ge(pT_mm, t + 1)
                nc.scalar.activation(probT[:, P * t:P * t + P], R[:, t, P:2 * P], ACT.Copy).then_inc(pT_up, 1)

            def yT(t):
                c = slice(P * t, P * t + P)
                act.wait_ge(y_mm, t + 1)
                nc.scalar.activation(yA[:, c], R[:, t, 2 * P:3 * P], ACT.Copy)
                nc.scalar.activation(yC[:, c], R[0:DC, t, 3 * P:4 * P], ACT.Copy).then_inc(y_up, 1)

            def xnT(t):
                act.wait_ge(t2_mm, t + 1)
                nc.scalar.activation(uABh[:, P * t:P * t + P], R[:, t, 2 * P:3 * P], ACT.Copy)
                nc.scalar.activation(uCh[:, P * t:P * t + P], R[:, t, 3 * P:4 * P], ACT.Copy).then_inc(xnh_up, 1)

            def phi_hi(_):
                act.wait_ge(phin_up, 1)
                nc.scalar.activation(phAh, phA[:, :], ACT.Copy)
                nc.scalar.activation(phCs[0:DC, :], phC[:, :], ACT.Copy).then_inc(phh_up, 1)

            def logits(t):
                act.wait_ge(lgm_up, t + 1)
                nc.scalar.activation(pe_exp[:, t, :], pe_exp[:, t, :], ACT.Exp).then_inc(lge_up, 1)
                act.wait_ge(nM_up, t + 1)
                nc.scalar.activation(tE[:, t, :], mE[:, t, :], ACT.Exp, bias=nM[:, t:t + 1]).then_inc(tE_up, 1)

            def slots_hi_first(half):
                slots_hi(0, half)

            turns((phi_squares, (8,)), (x1T, (6, 27, 40, 60)), (qk, (14, 38, 58, 75)), (values, (33, 51, 81, 89)),
                  (exps, (34, 47, 69, 93)), (phi_hi, (62,)), (pT, (50, 68, 80, 101)), (yT, (56, 72, 85, 105)),
                  (xnT, (87, 103, 111, 121)), (spread, (82, 112, 114, 137)), (logits, (108, 124, 128, 133)),
                  (slots_hi_first, (135, 143)), (lambda _: nc.scalar.preload_act_table(ACT.Gelu), (134,)),
                  (lambda _: w1_split(0, 0, 0, 0), (28,)), (lambda _: w1_split(1, 1, 1, 0), (42,)),
                  (lambda _: w2_split(0, 0, 0, 0), (122,)))
            act.wait_ge(gT_mm, NT)
            nc.scalar.activation(gateT[:, :], EO[0:E, 0, :], ACT.Copy).then_inc(gT_up, 1)
            gelu(0, 0, 0, 0)

            def body(j, first, last):
                for i in range(EG):
                    e = j * EG + i
                    more = not (last and i == EG - 1)
                    end = last and i == EG - 2
                    if not (last and i >= EG - 2):
                        w1_split(e + 2, i % 2, (i + 2) % EG, j + (i + 2) // EG)
                    if end:
                        w2_split(e + 1, (i + 1) % 2, (i + 1) % EG, j + (i + 1) // EG)
                    if more:
                        gelu(e + 1, (i + 1) % 2, (i + 1) % EG, j + (i + 1) // EG)
                    if more and not end:
                        w2_split(e + 1, (i + 1) % 2, (i + 1) % EG, j + (i + 1) // EG)
                    for r in range(2):
                        act.wait_ge(f2_bank, e * 2 + (r + 1))
                        wait(act, eo_add, e * 2 + (r - 1))
                        nc.scalar.activation(eol[:, r, :], EO[:, r, D:2 * D], ACT.Copy).then_inc(eo_cp, 1)
                        if r == 0:
                            if i == 1:
                                act.wait_ge(cwT_mm, j + 1)
                                wait(act, comb, j)
                                nc.scalar.activation(cwT[:, :], R[:, G, :], ACT.Copy).then_inc(cwT_up, 1)
                            if i == 2 and not last:
                                slots_hi(j + 1)

            groups(act, body)

        @block.vector
        def _(dve):
            links = [0]

            def link(ins):
                links[0] += 1
                ins.then_inc(link_s, 1)
                dve.wait_ge(link_s, links[0])

            def w1_split(e, par, slot, grp):
                dve.wait_ge(w1_hi, e * 2 + 1)
                nc.vector.tensor_tensor(w1l[:, par, :], rawA[:, slot, 0:H], w1h[:, par, :].bitcast(F32), ALU.subtract)
                dve.wait_ge(w1_hi, e * 2 + 2)
                nc.vector.tensor_tensor(w1c[DC:P, par, :], rawC[:, slot, :], w1c[0:DC, par, :].bitcast(F32),
                                        ALU.subtract).then_inc(w1_lo, 1)

            def w2_split(e, par, slot, grp):
                dve.wait_ge(w2_hi, e + 1)
                nc.vector.tensor_tensor(w2s[:, par, :, D:2 * D],
                                        rawA[:, slot, H:H + HT * D].rearrange("p (t d) -> p t d", t=HT),
                                        w2s[:, par, :, 0:D].bitcast(F32), ALU.subtract).then_inc(w2_lo, 1)

            def h_split(n, par):
                wait(dve, f2_bank, (n - 2) * 2 + 2 if not isinstance(n, int) or n >= 2 else 0)

                def hi(k):
                    dve.wait_ge(gelu_bank, n * 3 + (k + 1))
                    nc.vector.tensor_copy(hh[:, par, 2 * k:2 * k + 2, :], hidden(par, k)).then_inc(h_hi, 1)

                def lo(k):
                    nc.vector.tensor_tensor(hl[:, par, 2 * k:2 * k + 2, :], hidden(par, k),
                                            hh[:, par, 2 * k:2 * k + 2, :].bitcast(F32), ALU.subtract).then_inc(h_lo, 1)

                hi(0)
                dve.wait_ge(h_hi, n * 2 + 1)
                lo(0)
                hi(2)
                dve.wait_ge(h_hi1, n + 1)
                lo(1)
                dve.wait_ge(h_hi, n * 2 + 2)
                lo(2)

            def slots_lo(jj, half=None):
                for q in range(4) if half is None else (2 * half, 2 * half + 1):
                    hi, lo = ((xABh, xABl), (xCh, xCl))[q % 2]
                    dve.wait_ge(sl_hi, jj * 4 + (q + 1))
                    nc.vector.tensor_tensor(images(lo, q // 2), slot_bank(q), images(hi, q // 2).bitcast(F32),
                                            ALU.subtract).then_inc(sl_lo, 1)

            def stats1(t):
                if t == 0:
                    dve.wait_ge(bias_in, 32)
                dve.wait_ge(tok_mm, t + 1)
                link(nc.vector.tensor_tensor(h[:, t, :], R[:, t, 0:D], rb[:, 0, :], ALU.add))
                link(nc.vector.bn_stats(st[:, t, :], h[:, t, :]))
                link(nc.vector.bn_aggr(mv[:, t, :], st[:, t, :]))
                nc.vector.tensor_scalar(ve[:, t:t + 1], mv[:, t, 1:2], LN_EPS, None, ALU.add).then_inc(ve_up, 1)

            def norm1(t):
                dve.wait_ge(rstd_up, t + 1)
                nc.vector.tensor_scalar(xn[:, t, :], h[:, t, :], mv[:, t, 0:1], rstd[:, t:t + 1], ALU.subtract,
                                        ALU.mult).then_inc(xn1_up, 1)

            def score_max(t):
                dve.wait_ge(sc_mm, t + 1)
                for a in range(2):
                    r = slice(L * a, L * a + L)
                    x = nc.vector.tensor_reduce(nmx[r, t:t + 1], R[r, t, L * a:L * a + L], AX.X, ALU.max, negate=True)
                x.then_inc(nmx_up, 1)

            def probs(t):
                dve.wait_ge(exp_up, t + 1)
                link(nc.vector.reciprocal(arec[:, t:t + 1], asum[:, t:t + 1]))
                nc.vector.tensor_scalar(prob[:, t, :], prob[:, t, :], arec[:, t:t + 1], None,
                                        ALU.mult).then_inc(prob_up, 1)

            def residual(t):
                dve.wait_ge(o_mm, t + 1)
                link(nc.vector.tensor_tensor(h[:, t, :], R[:, t, 0:D], h[:, t, :], ALU.add))
                link(nc.vector.bn_stats(st[:, t, :], h[:, t, :]))
                link(nc.vector.bn_aggr(mv[:, t, :], st[:, t, :]))
                link(nc.vector.tensor_scalar(ve[:, t:t + 1], mv[:, t, 1:2], L2_EPS2, L2_EPS2 * LN_EPS, ALU.mult, ALU.add))
                nc.vector.scalar_tensor_tensor(pw[:, t:t + 1], mv[:, t, 1:2], float(D), ve[:, t:t + 1], ALU.mult,
                                               ALU.max).then_inc(pw_up, 1)

            def norm2(t):
                dve.wait_ge(pwr_up, t + 1)
                nc.vector.tensor_scalar(xn[:, t, :], h[:, t, :], mv[:, t, 0:1], pwr[:, t:t + 1], ALU.subtract,
                                        ALU.mult).then_inc(xn2_up, 1)

            def bc(x):
                return x.unsqueeze(2).broadcast_to([P, E, S])

            def less_max(t):
                lg = logit_banks(t).rearrange("p a (e s) -> p (a e) s", s=S)
                if t == 0:
                    dve.wait_ge(tok_mm, NT)
                dve.wait_ge(lg_mm, t + 1)
                link(nc.vector.tensor_reduce(mE[:, t, :], lg, AX.X, ALU.max))
                nc.vector.tensor_tensor(pe_exp[:, t, :].rearrange("p (e s) -> p e s", s=S), lg, bc(mE[:, t, :]),
                                        ALU.subtract).then_inc(lgm_up, 1)
                nc.vector.tensor_reduce(nM[:, t:t + 1], mE[:, t, :], AX.X, ALU.max, negate=True).then_inc(nM_up, 1)

            def sums(t):
                dve.wait_ge(lge_up, t + 1)
                link(nc.vector.tensor_reduce(sE[:, t, :], pe_exp[:, t, :].rearrange("p (e s) -> p e s", s=S), AX.X,
                                             ALU.add))
                nc.vector.reciprocal(rE[:, t, :], sE[:, t, :]).then_inc(rE_up, 1)

            def phi_square_sum(_):
                dve.wait_ge(phsq_up, 1)
                nc.vector.tensor_tensor(phsq[0:DC, :], phsq[0:DC, :], phsqC, ALU.add).then_inc(phsum_up, 1)

            def phi_sums(_):
                dve.wait_ge(phss_mm, 1)
                nc.vector.tensor_scalar(pss[:, :], Y[:, 0, 0:E * S // P], L2_EPS2, None, ALU.max).then_inc(phss_up, 1)

            def phi_diagonals(_):
                dve.wait_ge(pinv_up, 1)
                dve.wait_ge(bias_in, 32)
                dve.wait_ge(id_up, 2)
                link(nc.vector.tensor_scalar(pss[:, :], pinv[:, :], scl[:, 0:1], None, ALU.mult))
                nc.vector.tensor_tensor(dsc, ident[:, :].unsqueeze(1).broadcast_to([P, E * S // P, P]),
                                        pss[:, :].unsqueeze(2).broadcast_to([P, E * S // P, P]),
                                        ALU.mult).then_inc(dsc_up, 1)

            def phi_scale(_):
                dve.wait_ge(dsc_mm, 1)
                flat = Y[:, :, :].rearrange("p a n -> p (a n)")
                nc.vector.tensor_tensor(phA[:, :], flat, phA[:, :], ALU.mult)
                nc.vector.tensor_tensor(phC[:, :], flat[0:DC, :], phC[:, :], ALU.mult).then_inc(phin_up, 1)

            def phi_lo(_):
                dve.wait_ge(phh_up, 1)
                nc.vector.tensor_tensor(phCs[DC:P, :], phC[:, :], phCs[0:DC, :].bitcast(F32),
                                        ALU.subtract).then_inc(phlC_up, 1)

            def xnT_lo(t):
                c = slice(P * t, P * t + P)
                dve.wait_ge(xnh_up, t + 1)
                nc.vector.tensor_tensor(uABl[:, c], R[:, t, 2 * P:3 * P], uABh[:, c].bitcast(F32), ALU.subtract)
                nc.vector.tensor_tensor(uCl[:, c], R[:, t, 3 * P:4 * P], uCh[:, c].bitcast(F32),
                                        ALU.subtract).then_inc(xnT_up, 1)

            def gates(_):
                dve.wait_ge(tE_up, NT)
                dve.wait_ge(rE_up, NT)
                link(nc.vector.tensor_tensor(uE[:, :, :], sE[:, :, :], tE[:, :, :], ALU.mult))
                link(nc.vector.tensor_reduce(uS[:, :], uE[:, :, :], AX.X, ALU.add))
                link(nc.vector.reciprocal(ru[:, :], uS[:, :]))
                rub = ru[:, :].unsqueeze(2).broadcast_to([P, NT, E])
                nc.vector.tensor_tensor(gate[:, :, :], uE[:, :, :], rub, ALU.mult)
                nc.vector.tensor_tensor(gexp[:, :, :], tE[:, :, :], rub, ALU.mult).then_inc(gate_up, 1)

            def slots_lo_first(half):
                slots_lo(0, half)

            turns((phi_square_sum, (11,)), (stats1, (2, 10, 20, 24)), (norm1, (4, 15, 30, 41)), (phi_sums, (30,)),
                  (phi_diagonals, (36,)), (phi_scale, (53,)), (score_max, (19, 44, 66, 90)),
                  (probs, (45, 52, 73, 95)), (phi_lo, (79,)), (residual, (67, 84, 94, 109)),
                  (norm2, (77, 97, 98, 115)), (xnT_lo, (92, 107, 117, 123)), (less_max, (100, 119, 125, 129)),
                  (sums, (112, 127, 132, 136)), (gates, (141,)), (slots_lo_first, (138, 144)),
                  (lambda _: w1_split(0, 0, 0, 0), (46,)), (lambda _: w1_split(1, 1, 1, 0), (61,)),
                  (lambda _: w2_split(0, 0, 0, 0), (142,)))
            h_split(0, 0)

            def body(j, first, last):
                for i in range(EG):
                    e = j * EG + i
                    more = not (last and i == EG - 1)
                    end = last and i == EG - 2
                    if not (last and i >= EG - 2):
                        w1_split(e + 2, i % 2, (i + 2) % EG, j + (i + 2) // EG)
                    if end:
                        w2_split(e + 1, (i + 1) % 2, (i + 1) % EG, j + (i + 1) // EG)
                    if more:
                        h_split(e + 1, (i + 1) % 2)
                    if more and i != 2:
                        w2_split(e + 1, (i + 1) % 2, (i + 1) % EG, j + (i + 1) // EG)
                    for r in range(2):
                        dve.wait_ge(eo_cp, e * 2 + (r + 1))
                        if not (first and i == 0):
                            dve.wait_ge(eo_in[(i - 1) % EG], (j + 1 if i else j) * EO_IN)
                        nc.vector.tensor_tensor(eot[:, r, :], EO[:, r, 0:D], eol[:, r, :], ALU.add).then_inc(eo_add, 1)
                        if r == 0 and i == 2 and not last:
                            slots_lo(j + 1)
                            w2_split(e + 1, (i + 1) % 2, (i + 1) % EG, j + (i + 1) // EG)

            groups(dve, body)
            for t in range(2):
                if t == 0:
                    dve.wait_ge(half_comb, 1)
                else:
                    dve.wait_ge(comb, NG)
                nc.vector.tensor_tensor(xn[:, 2 * t:2 * t + 2, :],
                                        Y[:, t, 0:2 * D].rearrange("p (a d) -> p a d", a=2),
                                        h[:, 2 * t:2 * t + 2, :], ALU.add).then_inc(fin_up, 1)

        @block.tensor
        def _(pe):
            mm = nc.tensor.matmul

            pe.wait_ge(const_up, 1)
            for _ in range(WARM_UP):
                mm(R[:, 0, 0:P], ones[:, :], ones[:, :], start=True, stop=True)

            def phi_norms(q):
                if q == 0:
                    pe.wait_ge(phsum_up, 1)
                    pe.wait_ge(const_up, 4)
                for c in (2 * q, 2 * q + 1):
                    x = mm(Y[:, 0, c:c + 1], phsq[:, P * c:P * c + P], ones[:, 0:1], start=True, stop=True)
                if q == 3:
                    x.then_inc(phss_mm, 1)

            def bias(bank, k):
                return mm(bank, ones[0:1, :], rb[0:1, k, :], start=False, stop=True)

            def tok(t):
                pe.wait_ge(tok_in[t], 16)
                if t == 0:
                    pe.wait_ge(wtok_in, 16)
                for k in range(PK):
                    x = mm(R[:, t, 0:D], xTs[:, k, P * t:P * t + P], wtk[:, k, :], start=(k == 0), stop=(k == PK - 1))
                x.then_inc(tok_mm, 1)

            def transposes(bank, src, t, done):
                nc.tensor.transpose(bank[:, 0:P], src[:, t, 0:P], ident[:, :])
                nc.tensor.transpose(bank[0:DC, P:2 * P], src[:, t, P:D], ident[:, :]).then_inc(done, 1)

            def phi_spread(_):
                pe.wait_ge(dsc_up, 1)
                for c in range(E * S // P):
                    x = mm(Y[:, c // 4, P * (c % 4):P * (c % 4) + P], ones[:, :], dsc[:, c, :], start=True, stop=True)
                x.then_inc(dsc_mm, 1)

            def t1(t):
                pe.wait_ge(xn1_up, t + 1)
                wait(pe, v_up, t - 1)
                transposes(EO[:, t % 2, 0:2 * P], xn, t, t1_mm)

            def qk(t):
                c = slice(P * t, P * t + P)
                pe.wait_ge(x1T_up, t + 1)
                pe.wait_ge(attn_in, 64)
                for w in range(3):
                    o, cols = R[:, t, P * w:P * w + P], slice(P * w, P * w + P)
                    mm(o, wat[:, cols], xT2[:, 0, c], start=True, stop=False)
                    x = mm(o, watC[:, cols], xT2[0:DC, 1, c], start=False, stop=True)
                x.then_inc(qk_mm, 1)

            def vv(t):
                c = slice(P * t, P * t + P)
                pe.wait_ge(x1T_up, t + 1)
                pe.wait_ge(attn_in, 64)
                if t == 0:
                    pe.wait_ge(bias_in, 32)
                bank = EO[:, t % 2, 2 * P:2 * P + D]
                mm(bank, xT2[:, 0, c], wat[:, 2 * D:3 * D], start=True, stop=False)
                mm(bank, xT2[0:DC, 1, c], watC[:, 2 * D:3 * D], start=False, stop=False)
                bias(bank, 1).then_inc(v_mm, 1)

            def scores(t):
                c = slice(P * t, P * t + P)
                pe.wait_ge(qk_up, t + 1)
                mm(R[:, t, 0:P], qA[:, c], kA[:, c], start=True, stop=False)
                mm(R[:, t, 0:P], qC[:, c], kC[:, c], start=False, stop=True).then_inc(sc_mm, 1)

            def pT(t):
                pe.wait_ge(prob_up, t + 1)
                nc.tensor.transpose(R[:, t, P:2 * P], prob[:, t, :], ident[:, :]).then_inc(pT_mm, 1)

            def yT(t):
                c = slice(P * t, P * t + P)
                pe.wait_ge(pT_up, t + 1)
                pe.wait_ge(v_up, t + 1)
                mm(R[:, t, 2 * P:3 * P], v[:, t, 0:P], probT[:, c], start=True, stop=True)
                mm(R[0:DC, t, 3 * P:4 * P], v[:, t, P:D], probT[:, c], start=True, stop=True).then_inc(y_mm, 1)

            def proj(t):
                c = slice(P * t, P * t + P)
                pe.wait_ge(y_up, t + 1)
                bank = R[:, t, 0:D]
                mm(bank, yA[:, c], wat[:, 3 * D:4 * D], start=True, stop=False)
                mm(bank, yC[:, c], watC[:, 3 * D:4 * D], start=False, stop=False)
                bias(bank, 2).then_inc(o_mm, 1)

            def t2(t):
                pe.wait_ge(xn2_up, t + 1)
                mm(R[DC:P, t, 3 * P:4 * P], xn[:, t, P:D], ident[:, :], start=True, stop=True)
                transposes(R[:, t, 2 * P:4 * P], xn, t, t2_mm)

            def logits(t):
                c = slice(P * t, P * t + P)
                if t == 0:
                    pe.wait_ge(phlA_up, 1)
                    pe.wait_ge(phlC_up, 1)
                pe.wait_ge(xnT_up, t + 1)
                if t == 2:
                    pe.wait_ge(v_up, NT)
                else:
                    wait(pe, lgm_up, min(t, 2))
                for a in range(2):
                    bank = logit_banks(t)[:, a, :]
                    n = slice(512 * a, 512 * a + 512)
                    mm(bank, uABh[:, c], phAh[:, n], start=True, stop=False)
                    mm(bank, uABh[:, c], phAl[:, n], start=False, stop=False)
                    mm(bank, uABl[:, c], phAh[:, n], start=False, stop=False)
                    mm(bank, uCh[:, c], phCs[:, n], start=False, stop=False)
                    x = mm(bank, uCl[:, c], phCs[:, n], start=False, stop=True)
                x.then_inc(lg_mm, 1)

            def slots(jj, half=None):
                for q in range(4) if half is None else (2 * half, 2 * half + 1):
                    if q % 2 == 0:
                        pe.wait_ge(dwn_up, jj * NT + (q + 2))
                    part = (slice(0, P), slice(P, 2 * P))[q % 2]
                    if q == 0:
                        wait(pe, cwT_up, jj)
                    else:
                        wait(pe, gelu_bank, jj * 12 + (q - 3))
                    for b in range(4):
                        bi = 4 * (q // 2) + b
                        x = mm(R[:, (G, 0, 1, 2)[q], GC * b:GC * b + GC], xnp[:, bi, part],
                               dwn[:, bi // 2, :], start=True, stop=True)
                    x.then_inc(sl_mm, 1)

            def slots_first(half):
                if half == 0:
                    pe.wait_ge(xnT_up, NT)
                pe.wait_ge(xnp_up, 4 * half + 4)
                slots(0, half)

            turns((tok, (1, 7, 12, 21)), (t1, (5, 25, 37, 55)), (phi_norms, (16, 18, 23, 26)), (phi_spread, (43,)),
                  (qk, (9, 32, 49, 65)), (vv, (29, 39, 57, 71)), (scores, (17, 42, 64, 86)),
                  (pT, (48, 63, 77, 99)), (yT, (54, 70, 83, 102)), (proj, (59, 78, 88, 106)),
                  (t2, (84, 100, 104, 118)), (logits, (94, 110, 120, 126)), (slots_first, (131, 140)))

            def f1(n, par, slot):
                pe.wait_ge(w1_lo, n + 1)
                for k in range(3):
                    wait(pe, gelu_bank, (n - 1) * 3 + (k + 1) if not isinstance(n, int) or n >= 1 else 0)
                    for m in range(2):
                        t = 2 * k + m
                        c = slice(P * t, P * t + P)
                        o = R[:, k, m * ROWS:(m + 1) * ROWS]
                        mm(o, w1h[:, par, c], xABh[:, slot, :], start=True, stop=False)
                        mm(o, w1h[:, par, c], xABl[:, slot, :], start=False, stop=False)
                        mm(o, w1l[:, par, c], xABh[:, slot, :], start=False, stop=False)
                        mm(o, w1c[:, par, c], xCh[:, slot, :], start=False, stop=False)
                        x = mm(o, w1c[:, par, c], xCl[:, slot, :], start=False, stop=True)
                    x.then_inc(f1_bank, 1)

            def f2(e, par, r):
                if r == 0:
                    pe.wait_ge(h_lo, e * 3 + 3)
                    pe.wait_ge(w2_lo, e + 1)
                wait(pe, eo_add, e * 2 + (r - 1))
                for t in range(HT):
                    rows = slice(P * r, P * r + P)
                    mm(EO[:, r, 0:2 * D], hh[:, par, t, rows], w2s[:, par, t, :], start=(t == 0), stop=False)
                    x = mm(EO[:, r, 0:D], hl[:, par, t, rows], w2s[:, par, t, 0:D], start=False, stop=(t == HT - 1))
                x.then_inc(f2_bank, 1)

            def combine(j, last):
                pe.wait_ge(cwT_up, j + 1)
                for experts in ((range(EG - 1), range(EG - 1, EG)) if last else (range(EG),)):
                    for i in experts:
                        pe.wait_ge(eo_in[i], j * EO_IN + EO_IN)
                    rows = slice(S * experts[0], S * (experts[-1] + 1))
                    for b in range(B):
                        half, at = L * (b % 2), D * ((b // 2) % 2)
                        x = mm(Y[half:half + L, b // 4, at:at + D], cwT[rows, L * b:L * b + L], eog[rows, b, :],
                               start=False, stop=last and experts[-1] == EG - 1, skip_group_check=True)
                        if last and experts[-1] == EG - 1 and b == B // 2 - 1:
                            x.then_inc(half_comb, 1)
                x.then_inc(comb, 1)

            pe.wait_ge(gate_up, 1)
            for t in range(NT):
                nc.tensor.transpose(EO[0:E, 0, P * t:P * t + P], gate[:, t, :], ident[:, :]).then_inc(gT_mm, 1)
            pe.wait_ge(sl_lo, 4)
            f1(0, 0, 0)
            pe.wait_ge(gT_up, 1)
            pe.wait_ge(b2_in, 16)
            for t in range(NT):
                mm(Y[:, t // 2, D * (t % 2):D * (t % 2) + D], gateT[:, P * t:P * t + P], b2s[:, :],
                   start=(t % 2 == 0), stop=False, skip_group_check=True)

            def body(j, first, last):
                for i in range(EG):
                    e = j * EG + i
                    if not (last and i == EG - 1):
                        if i == EG - 1:
                            pe.wait_ge(sl_lo, j * 4 + 8)
                        f1(e + 1, (i + 1) % 2, (i + 1) % EG)
                    f2(e, i % 2, 0)
                    if i == 0 and not first:
                        combine(j - 1, False)
                    if i == 1:
                        pe.wait_ge(cws_up, j + 1)
                        pe.wait_ge(sl_lo, j * 4 + 4)
                        for t in range(NT):
                            x = nc.tensor.transpose(R[:, G, P * t:P * t + P], cws[:, t, :], ident[:, :])
                        x.then_inc(cwT_mm, 1)
                    if i == 2 and not last:
                        slots(j + 1)
                    f2(e, i % 2, 1)

            groups(pe, body)
            combine(NG - 1, True)


_INS = ["xT", "wtokT", "rowbias", "wattnAB", "wattnC", "bqkAB", "bqkC", "phi", "scale", "b2", "wA", "wC"]


def kernel(**inputs):
    import numpy as np
    import concourse.bacc as bacc
    from concourse.bass_utils import run_bass_kernel_spmd

    def t(name):
        return np.asarray(inputs[name])

    x = t("x").reshape(B, 3, L, 2, P).transpose(4, 1, 3, 0, 2).reshape(P, PK, B * L)
    wtok = t("L0_tok_W").T.reshape(PK, P, D).transpose(1, 0, 2)
    wq, wk, wv, wo = (t(f"L0_attn_w{c}").T for c in "qkvo")
    attn = np.concatenate([wq[:, :P], wk[:, :P], wq[:, P:], wk[:, P:], wv, wo], axis=1)
    bqk = np.stack([t("L0_attn_bq"), t("L0_attn_bk")], axis=1)
    w1, b1, w2 = t("L0_ffn_w1"), t("L0_ffn_b1"), t("L0_ffn_w2")
    w2p = w2.reshape(E, HT, P, D).transpose(0, 2, 1, 3).reshape(E, P, HT * D)
    b1p = b1.reshape(E, HT, P).transpose(0, 2, 1)
    arrays = {
        "xT": x,
        "wtokT": wtok,
        "rowbias": np.stack([t("L0_tok_b"), t("L0_attn_bv"), t("L0_attn_bo")]),
        "wattnAB": attn[:P],
        "wattnC": attn[P:],
        "bqkAB": bqk[:P],
        "bqkC": bqk[P:],
        "phi": t("L0_ffn_phi").reshape(D, E * S),
        "scale": t("L0_ffn_scale"),
        "b2": t("L0_ffn_b2"),
        "wA": np.concatenate([w1[:, :P, :], w2p, b1p], axis=2),
        "wC": w1[:, P:, :],
    }
    arrays = {k: np.ascontiguousarray(a) for k, a in arrays.items()}
    nc = bacc.Bacc("TRN2", target_bir_lowering=False, num_devices=1)
    args = [nc.dram_tensor(f"{k}_dram", arrays[k].shape, mybir.dt.from_np(arrays[k].dtype), kind="ExternalInput").ap()
            for k in _INS]
    args.append(nc.dram_tensor("out_dram", (B, L, D), F32, kind="ExternalOutput").ap())
    vit_block(nc, *args)
    r = run_bass_kernel_spmd(nc, [{f"{k}_dram": arrays[k] for k in _INS}], core_ids=[0])
    return r.results[0]["out_dram"]
```
